# Optimizing a Trainium2 kernel written in Bass

```python
import numpy as np
import jax
import jax.numpy as jnp

def _softmax(x, axis=-1):
    return jax.nn.softmax(x, axis=axis)

def _gelu(x):
    return jax.nn.gelu(x, approximate=True)

def _silu(x):
    return jax.nn.silu(x)

def _sigmoid(x):
    return jax.nn.sigmoid(x)

def _layernorm(x, axis=-1, eps=1e-05):
    m = jnp.mean(x, axis=axis, keepdims=True)
    v = jnp.var(x, axis=axis, keepdims=True)
    return (x - m) / jnp.sqrt(v + eps)

def _scatter_add(tgt, idx, src, axis=0):
    return tgt.at[idx].add(src)

def _segment_sum(src, seg, n):
    return jax.ops.segment_sum(src, seg, n)
kernel_name = 'mk_cond_resid_d1_seqx_r2_7c2c72'

def setup_inputs(seed: int=0):
    np.random.seed(seed)
    _w = jnp.asarray

    def _rec_inputs():
        import jax
        import jax.numpy as jnp
        _rk = jax.random.key(seed)
        x = 7.22e-05 + 1 * jax.random.normal(jax.random.fold_in(_rk, 1), (32, 512, 512), jnp.float32)
        _lenS = 512 - jax.random.randint(jax.random.fold_in(_rk, 7), (32,), 0, max(1, 512 // 4) + 1, jnp.int32)
        _lenS2 = 512 - jax.random.randint(jax.random.fold_in(_rk, 8), (32,), 0, max(1, 512 // 4) + 1, jnp.int32)
        cond_512 = 0.0061147 + 1.02565 * jax.random.normal(jax.random.fold_in(_rk, 11), (32, 256), jnp.float32)
        return (x, cond_512)
    x, cond_512 = _rec_inputs()

    def _L0_cond_setup():
        import jax, jax.numpy as jnp
        import numpy as np
        import math
        HEAD_NUM = 16
        EPS = 1e-08

        def modulated_linear(x, s, aff_w, aff_b, w, b):
            style = s @ aff_w.T + aff_b
            w_mod = w[None, :, :] * style[:, None, :]
            demod = jax.lax.rsqrt(jnp.sum(w_mod * w_mod, axis=2) + EPS)
            w_mod = w_mod * demod[:, :, None]
            return jnp.einsum('bni,boi->bno', x, w_mod) + b
        key = jax.random.key(seed)
        ks = jax.random.split(key, 6)
        B, N, F, S = (8, 512, 512, 256)
        return {'x': jax.random.normal(ks[0], (B, N, F), dtype=jnp.float32), 's': jax.random.normal(ks[1], (B, S), dtype=jnp.float32), 'k_aff_w': jax.random.normal(ks[2], (F, S), dtype=jnp.float32) * 0.02, 'k_aff_b': jnp.ones((F,), dtype=jnp.float32), 'k_w': jax.random.normal(ks[3], (F, F), dtype=jnp.float32) * 0.02, 'k_b': jnp.zeros((F,), dtype=jnp.float32), 'o_aff_w': jax.random.normal(ks[4], (F, S), dtype=jnp.float32) * 0.02, 'o_aff_b': jnp.ones((F,), dtype=jnp.float32), 'o_w': jax.random.normal(ks[5], (F, F), dtype=jnp.float32) * 0.02, 'o_b': jnp.zeros((F,), dtype=jnp.float32)}
    _L0_cond_all = _L0_cond_setup()
    _L0_cond_in = {k: v for k, v in _L0_cond_all.items() if k in ('k_aff_w', 'k_aff_b', 'k_w', 'k_b', 'o_aff_w', 'o_aff_b', 'o_w', 'o_b')}
    del _L0_cond_all
    return {'x': x, 'cond_512': cond_512, 'L0_cond_k_aff_w': _L0_cond_in['k_aff_w'], 'L0_cond_k_aff_b': _L0_cond_in['k_aff_b'], 'L0_cond_k_w': _L0_cond_in['k_w'], 'L0_cond_k_b': _L0_cond_in['k_b'], 'L0_cond_o_aff_w': _L0_cond_in['o_aff_w'], 'L0_cond_o_aff_b': _L0_cond_in['o_aff_b'], 'L0_cond_o_w': _L0_cond_in['o_w'], 'L0_cond_o_b': _L0_cond_in['o_b']}

def reference(x, cond_512, L0_cond_k_aff_w, L0_cond_k_aff_b, L0_cond_k_w, L0_cond_k_b, L0_cond_o_aff_w, L0_cond_o_aff_b, L0_cond_o_w, L0_cond_o_b):
    import jax
    import jax.numpy as jnp

    def _L0_cond_ref(x, s, k_aff_w, k_aff_b, k_w, k_b, o_aff_w, o_aff_b, o_w, o_b):
        import jax, jax.numpy as jnp
        import numpy as np
        import math
        HEAD_NUM = 16
        EPS = 1e-08

        def modulated_linear(x, s, aff_w, aff_b, w, b):
            style = s @ aff_w.T + aff_b
            w_mod = w[None, :, :] * style[:, None, :]
            demod = jax.lax.rsqrt(jnp.sum(w_mod * w_mod, axis=2) + EPS)
            w_mod = w_mod * demod[:, :, None]
            return jnp.einsum('bni,boi->bno', x, w_mod) + b
        B, N, F = x.shape
        H = HEAD_NUM
        D = F // H
        kx = modulated_linear(x, s, k_aff_w, k_aff_b, k_w, k_b)
        kx = kx.reshape(B, N, H, D)
        q = k = v = kx
        scores = jnp.einsum('bnhd,bnjd->bnhj', q, k) / math.sqrt(D)
        A = jax.nn.softmax(scores, axis=-1)
        out = jnp.einsum('bnhj,bnjd->bnhd', A, v).reshape(B, N, F)
        out = modulated_linear(out, s, o_aff_w, o_aff_b, o_w, o_b)
        return out
    x = x + _L0_cond_ref(x, cond_512, L0_cond_k_aff_w, L0_cond_k_aff_b, L0_cond_k_w, L0_cond_k_b, L0_cond_o_aff_w, L0_cond_o_aff_b, L0_cond_o_w, L0_cond_o_b)
    return x

_drawn_inputs = setup_inputs


def setup_inputs(seed=0):
    import zlib

    import numpy as np

    out = dict(_drawn_inputs(seed))
    spreads = {'L0_cond_k_aff_b': (1.0, 0.2),
     'L0_cond_k_b': (0.0, 0.1),
     'L0_cond_o_aff_b': (1.0, 0.2),
     'L0_cond_o_b': (0.0, 0.1)}
    factors = {}
    for name, (base, spread) in spreads.items():
        noise = np.random.default_rng([zlib.crc32(name.encode()), seed]).standard_normal(out[name].shape)
        drawn = base * np.exp(spread * noise) if base else spread * noise
        out[name] = jnp.asarray(drawn.astype(out[name].dtype))
    for name, factor in factors.items():
        out[name] = (out[name] * factor).astype(out[name].dtype)
    return out
```

```python
from contextlib import ExitStack

import concourse.bass as bass
from concourse import mybir
from concourse.alu_op_type import AluOpType as ALU

F32 = mybir.dt.float32
ACT = mybir.ActivationFunctionType
AX_X = mybir.AxisListType.X

P = 128
B, N, F, S = 32, 512, 512, 256
H, D = 16, 32
C = F // P
HC = H // C
G = N // P
U = P // 8
Q = 4
SC = S // P
SLOTS = 4
SCALE = float(D) ** -0.5
EPS = 1e-8
DMA = 16


class Step:

    def __init__(self, lap, j, n=None):
        self.lap, self.j, self.n = lap, j, n
        self.a = n is None or n < B
        self.b = n is None or 1 <= n <= B
        self.c = n is None or n >= 2

    def batch(self, back=0):
        return self.lap * SLOTS + (self.j - back)

    def times(self, per, back=0, more=0):
        return self.lap * (SLOTS * per) + (per * (self.j - back) + more)

    def first(self, n):
        return self.n is not None and self.n < n

    def laps(self, back=0):
        return self.lap + ((self.j - back) // SLOTS + 1)


def wait(eng, sem, value):
    if not isinstance(value, int) or value > 0:
        eng.wait_ge(sem, value)


def run_steps(eng, step, laps=B // SLOTS):
    for n in range(SLOTS):
        step(Step(n // SLOTS, n % SLOTS, n))
    with eng.Fori(1, laps) as lap:
        for j in range(SLOTS):
            step(Step(lap, j))
    for n in range(SLOTS * laps, B + 2):
        step(Step(n // SLOTS, n % SLOTS, n))


def build(nc, x, cond_t, k_aff_t, k_aff_b, k_w_t, k_b, o_aff_t, o_aff_b, o_w_t, o_b, ident_in, mask_in, out, demod_dram):
    x_v = x.rearrange("b (g p) i -> b p g i", p=P)
    out_v = out.rearrange("b (g p) o -> b g p o", p=P)

    with ExitStack() as ctx:
        def sb(name, shape):
            return ctx.enter_context(nc.sbuf_tensor(name, shape, F32))

        def sem(name):
            return ctx.enter_context(nc.semaphore(name))

        ident = sb("ident", [P, P])
        mask = sb("mask", [P, 32])
        wk_t = sb("wk_t", [P, C, F])
        wo_t = sb("wo_t", [P, C, F])
        o_bias = sb("o_bias", [P, F])
        k_bias = sb("k_bias", [P, C])
        factors = sb("factors", [P, B, 3 * C])
        cur = sb("cur", [P, SLOTS, 3 * C])
        demod_o = sb("demod_o", [P, 2, F])

        xs = sb("xs", [P, SLOTS, G, F])
        xt = sb("xt", [P, C, N])
        ks = sb("ks", [P, C, N])
        kt_in = sb("kt_in", [P, H, P])
        kt = sb("kt", [P, P, H])
        vs = sb("vs", [P, U, P])
        sm = sb("sm", [P, 2, 512])
        pr = sb("pr", [P, 2, 512])
        mx = sb("mx", [P, 2, U])
        den = sb("den", [P, 2, U])
        rden = sb("rden", [P, 2, U])
        pt = sb("pt", [P, G, U, P])
        ot = sb("ot", [P, H, P])
        os_ = sb("os_", [P, C, N])
        wo_b = sb("wo_b", [P, C, F])

        names = """loaded aff_ready x_ready0 x_ready1 x_ready2 x_ready3 kt_landed
            ot_ready0 ot_ready1 ot_ready2 ot_ready3 demod_row0 demod_row1 demod_stored stored0 stored1
            stored2 stored3
            setup_ps setup_dve setup_act zeroed
            xt_ps k_ps v_ps s_ps av_ps o_ps
            cur_ready kt_ready xt_ready ks_ready vs_ready exp_ready ot_done
            s_read shifted pt_ready o_ready max_ready sum_ready inv_ready prob_ready x_bias_ready wo_scaled wo_ready""".split()
        s = {name: sem(name) for name in names}
        x_ready = [s[f"x_ready{j}"] for j in range(SLOTS)]
        stored = [s[f"stored{j}"] for j in range(SLOTS)]
        ot_ready = [s[f"ot_ready{g}"] for g in range(G)]
        demod_row = [s["demod_row0"], s["demod_row1"]]

        def bank_pair(name):
            return ctx.enter_context(nc.psum_tensor(name, [P, 2, 512], F32))

        ps_t = bank_pair("ps_t")
        ps_p = bank_pair("ps_p")
        ps_s = bank_pair("ps_s")
        ps_a = bank_pair("ps_a")

        setup(nc, ctx, sb, s, x_v, cond_t, k_aff_t, k_aff_b, k_w_t, k_b, o_aff_t, o_aff_b, o_w_t, o_b, ident_in, mask_in,
              demod_dram, ident, mask, wk_t, wo_t, o_bias, k_bias, factors, xs, pt, vs, x_ready, ps_t, ps_p, ps_s)

        block = ctx.enter_context(nc.Block())

        @block.sync
        def _(sp):
            def early(value):
                if not isinstance(value, int):
                    sp.lower_val(value)
                return value

            def address(ap):
                early(ap.offset * 4)
                return ap

            def step(st):
                j = st.j
                if st.n is None or 1 <= st.n <= B:
                    row = address(demod_dram[st.batch(1), :].partition_broadcast(P))
                    wait(sp, s["wo_ready"], st.times(1, 2))
                    sp.dma_start(demod_o[:, (j - 1) % 2, :], row).then_inc(demod_row[(j - 1) % 2], DMA)
                if st.n is None or st.n < B - 1:
                    x_next = address(x_v[st.batch(-1)])
                if st.n is None or 3 <= st.n < B - 1:
                    sp.wait_ge(stored[(j + 1) % SLOTS], st.laps(3) * (G * DMA))
                if st.n is None or st.n < B - 1:
                    sp.dma_start(xs[:, (j + 1) % SLOTS, :, :], x_next).then_inc(x_ready[(j + 1) % SLOTS], DMA)
                if st.c:
                    early(st.times(4, 2))
                    sp.wait_ge(s["ot_done"], st.times(4, 2, 4))
                    wait(sp, s["o_ps"], st.times(4, 2))
                    for g in range(G):
                        for hh in range(HC):
                            sp.dma_start(os_[32 * hh:32 * hh + 32, :, P * g:P * g + P],
                                         ot[32 * g:32 * g + 32, hh:H:HC, :]).then_inc(ot_ready[g], DMA)
                if st.a:
                    sp.wait_ge(s["ks_ready"], st.times(4, 0, 4))
                    wait(sp, s["kt_ready"], st.times(4, 0))
                    for hh in range(HC):
                        for g in range(G):
                            sp.dma_start(kt_in[32 * g:32 * g + 32, hh:H:HC, :],
                                         ks[32 * hh:32 * hh + 32, :, P * g:P * g + P]).then_inc(s["kt_landed"], DMA)
                if st.c:
                    for g in range(G):
                        rows = address(out_v[st.batch(2), g])
                        sp.wait_ge(s["o_ready"], st.times(4, 2, g + 1))
                        sp.dma_start(rows, xs[:, (j - 2) % SLOTS, g, :]).then_inc(stored[(j - 2) % SLOTS], DMA)

            run_steps(sp, step, B // SLOTS - 1)
            for j in range(SLOTS):
                sp.wait_ge(stored[j], (B // SLOTS) * G * DMA)

        @block.tensor
        def _(pe):
            def attention_out(st):
                pe.wait_ge(s["pt_ready"], st.times(4, 2, 4))
                pe.wait_ge(s["vs_ready"], st.times(4, 2, 4))
                for k in range(4):
                    wait(pe, s["ot_done"], st.times(4, 2, k - 1))
                    for ul in range(4):
                        for g in range(G):
                            u = 4 * k + ul
                            last = nc.tensor.matmul(ps_a[32 * g:32 * g + 32, k % 2, P * ul:P * ul + P],
                                                    vs[:, u, 32 * g:32 * g + 32], pt[:, g, u, :],
                                                    start=True, stop=True)
                    last.then_inc(s["av_ps"], 1)

            def v_rows(st):
                for k in range(4):
                    if k == 0:
                        wait(pe, s["s_read"], st.times(4, 1, -1))
                    pe.wait_ge(s["kt_ready"], st.times(4, 1, k + 1))
                    if k < 2:
                        wait(pe, s["xt_ready"], st.times(4, 1, 3 + k))
                    else:
                        wait(pe, s["vs_ready"], st.times(4, 1, k - 1))
                    for ul in range(4):
                        u = 4 * k + ul
                        last = nc.tensor.transpose(ps_t[:, k % 2, P * ul:P * ul + P],
                                                   kt[:, 8 * u:8 * u + 8, :].rearrange("p t h -> p (t h)"), ident[:, :])
                    last.then_inc(s["v_ps"], 1)

            def scores(st, g):
                for u in range(U):
                    for q in range(Q):
                        t = 8 * u + 2 * q
                        rows = kt[32 * g:32 * g + 32, t:t + 2, :].rearrange("p t h -> p (t h)")
                        last = nc.tensor.matmul(ps_s[32 * q:32 * q + 32, g % 2, 32 * u:32 * u + 32], rows, rows,
                                                start=True, stop=True)
                last.then_inc(s["s_ps"], 1)

            def x_transposes(st):
                pe.wait_ge(x_ready[st.j], st.laps() * DMA)
                for c in range(C):
                    if c < 2:
                        wait(pe, s["vs_ready"], st.times(4, 1, 3 + c))
                    else:
                        pe.wait_ge(s["xt_ready"], st.times(4, 0, c - 1))
                    for g in range(G):
                        last = nc.tensor.transpose(ps_t[:, c % 2, P * g:P * g + P],
                                                   xs[:, st.j, g, P * c:P * c + P], ident[:, :])
                    last.then_inc(s["xt_ps"], 1)

            def k_projection(st, c):
                if st.b and c < C - 1:
                    wait(pe, s["s_read"], st.times(4, 1, c))
                pe.wait_ge(s["xt_ready"], st.times(4, 0, 4))
                if c < 2:
                    if st.first(3):
                        wait(pe, s["ks_ready"], st.times(4, 0, c - 1))
                    else:
                        pe.wait_ge(s["o_ready"], st.times(4, 3, 3 + c))
                else:
                    pe.wait_ge(s["ks_ready"], st.times(4, 0, c - 1))
                for i in range(C):
                    last = nc.tensor.matmul(ps_p[:, c % 2, :], wk_t[:, i, P * c:P * c + P], xt[:, i, :],
                                            start=(i == 0), stop=(i == C - 1))
                last.then_inc(s["k_ps"], 1)

            def o_projection(st, g):
                if g == 0:
                    pe.wait_ge(s["wo_ready"], st.times(1, 2, 1))
                pe.wait_ge(ot_ready[g], st.times(HC * DMA, 2, HC * DMA))
                if g < 2:
                    if st.a:
                        pe.wait_ge(s["ks_ready"], st.times(4, 0, 3 + g))
                    else:
                        pe.wait_ge(s["o_ready"], st.times(4, 2, g - 1))
                else:
                    pe.wait_ge(s["o_ready"], st.times(4, 2, g - 1))
                for c in range(C):
                    last = nc.tensor.matmul(ps_p[:, g % 2, :], os_[:, c, P * g:P * g + P], wo_b[:, c, :],
                                            start=(c == 0), stop=(c == C - 1))
                last.then_inc(s["o_ps"], 1)

            def step(st):
                if st.c:
                    attention_out(st)
                if st.b:
                    v_rows(st)
                if st.a:
                    if st.b:
                        scores(st, 0)
                    x_transposes(st)
                    for c in range(C):
                        k_projection(st, c)
                        if st.b and c < C - 1:
                            scores(st, c + 1)
                elif st.b:
                    for g in range(G):
                        if g:
                            pe.wait_ge(s["s_read"], st.times(4, 1, g - 1))
                        scores(st, g)
                if st.c:
                    for g in range(G):
                        o_projection(st, g)

            run_steps(pe, step)

        @block.scalar
        def _(act):
            def step(st):
                j = st.j
                if st.b:
                    act.wait_ge(s["kt_landed"], st.times(H * DMA, 1, H * DMA))
                    wait(act, s["s_ps"], st.times(4, 1))
                    wait(act, s["v_ps"], st.times(4, 1))
                    for k in range(4):
                        nc.scalar.activation(kt[:, 32 * k:32 * k + 32, :],
                                             kt_in[:, :, 32 * k:32 * k + 32].rearrange("p h t -> p t h"),
                                             ACT.Copy).then_inc(s["kt_ready"], 1)
                if st.c:
                    for g in range(G):
                        wait(act, ot_ready[g], st.times(HC * DMA, 2))
                    for k in range(4):
                        act.wait_ge(s["av_ps"], st.times(4, 2, k + 1))
                        nc.scalar.activation(ot[:, :, 32 * k:32 * k + 32],
                                             ps_a[:, k % 2, :].rearrange("p (t h) -> p h t", h=H),
                                             ACT.Copy).then_inc(s["ot_done"], 1)
                if st.a:
                    wait(act, s["wo_ready"], st.times(1, 3))
                    nc.scalar.activation(cur[:, j, :], factors[:, st.batch(), :], ACT.Copy).then_inc(s["cur_ready"], 1)
                if st.b:
                    wait(act, s["av_ps"], st.times(4, 2, 4) if st.c else 0)
                    for k in range(4):
                        act.wait_ge(s["v_ps"], st.times(4, 1, k + 1))
                        nc.scalar.activation(vs[:, 4 * k:4 * k + 4, :], ps_t[:, k % 2, :].rearrange("p (u f) -> p u f", u=4),
                                             ACT.Copy).then_inc(s["vs_ready"], 1)

                def exps(g):
                    act.wait_ge(s["shifted"], st.times(4, 1, g + 1))
                    wait(act, s["pt_ready"], st.times(4, 1, g - 1))
                    nc.scalar.activation(pr[:, g % 2, :], sm[:, g % 2, :], ACT.Exp, scale=SCALE).then_inc(s["exp_ready"], 1)

                if st.a:
                    act.wait_ge(s["cur_ready"], st.times(1, 0, 1))
                    wait(act, s["k_ps"], st.times(4, 0))
                    for c in range(C):
                        act.wait_ge(s["xt_ps"], st.times(4, 0, c + 1))
                        nc.scalar.activation(xt[:, c, :], ps_t[:, c % 2, :], ACT.Copy,
                                             scale=cur[:, j, c:c + 1]).then_inc(s["xt_ready"], 1)
                if st.b:
                    exps(0)
                if st.a:
                    if not st.first(1):
                        act.wait_ge(s["kt_landed"], st.times(H * DMA, 0))
                    for c in range(C):
                        act.wait_ge(s["k_ps"], st.times(4, 0, c + 1))
                        nc.scalar.activation(ks[:, c, :], ps_p[:, c % 2, :], ACT.Identity, bias=k_bias[:, c:c + 1],
                                             scale=cur[:, j, C + c:C + c + 1]).then_inc(s["ks_ready"], 1)
                        if st.b and c < C - 1:
                            exps(c + 1)
                elif st.b:
                    for g in range(1, G):
                        exps(g)

            run_steps(act, step)

        @block.vector
        def _(dve):
            def scores_in(st, g):
                r = g % 2
                blocks = sm[:, r, :].rearrange("p (u f) -> p u f", u=U)
                dve.wait_ge(s["s_ps"], st.times(4, 1, g + 1))
                wait(dve, s["exp_ready"], st.times(4, 1, g - 1))
                nc.vector.tensor_tensor(blocks, ps_s[:, r, :].rearrange("p (u f) -> p u f", u=U),
                                        mask[:, :].unsqueeze(1).to_broadcast([P, U, 32]), ALU.add).then_inc(s["s_read"], 1)
                dve.wait_ge(s["s_read"], st.times(4, 1, g + 1))
                nc.vector.tensor_reduce(mx[:, r, :], blocks, AX_X, ALU.max).then_inc(s["max_ready"], 1)
                dve.wait_ge(s["max_ready"], st.times(4, 1, g + 1))
                nc.vector.tensor_tensor(blocks, blocks, mx[:, r, :].unsqueeze(2).to_broadcast([P, U, 32]),
                                        ALU.subtract).then_inc(s["shifted"], 1)

            def probabilities(st, g):
                r = g % 2
                blocks = pr[:, r, :].rearrange("p (u f) -> p u f", u=U)
                dve.wait_ge(s["exp_ready"], st.times(4, 1, g + 1))
                nc.vector.tensor_reduce(den[:, r, :], blocks, AX_X, ALU.add).then_inc(s["sum_ready"], 1)
                dve.wait_ge(s["sum_ready"], st.times(4, 1, g + 1))
                nc.vector.reciprocal(rden[:, r, :], den[:, r, :]).then_inc(s["inv_ready"], 1)
                dve.wait_ge(s["inv_ready"], st.times(4, 1, g + 1))
                nc.vector.tensor_tensor(blocks, blocks, rden[:, r, :].unsqueeze(2).to_broadcast([P, U, 32]),
                                        ALU.mult).then_inc(s["prob_ready"], 1)
                dve.wait_ge(s["prob_ready"], st.times(4, 1, g + 1))
                if g == 0 and st.c:
                    dve.wait_ge(s["av_ps"], st.times(4, 2, 4))
                for q in range(Q):
                    last = nc.vector.transpose(pt[32 * q:32 * q + 32, g, :, 32 * q:32 * q + 32],
                                               blocks[32 * q:32 * q + 32])
                last.then_inc(s["pt_ready"], 1)

            def step(st):
                if st.b:
                    scores_in(st, 0)
                    for g in range(G):
                        if g < G - 1:
                            scores_in(st, g + 1)
                        probabilities(st, g)
                if st.c:
                    dve.wait_ge(s["x_bias_ready"], st.times(1, 2, 1))
                    for g in range(G):
                        dve.wait_ge(s["o_ps"], st.times(4, 2, g + 1))
                        row = xs[:, (st.j - 2) % SLOTS, g, :]
                        nc.vector.tensor_tensor(row, ps_p[:, g % 2, :], row, ALU.add).then_inc(s["o_ready"], 1)

            run_steps(dve, step)

        @block.gpsimd
        def _(pool):
            def step(st):
                j = st.j
                if st.c:
                    wait(pool, s["o_ps"], st.times(4, 2))
                    r = (j - 2) % 2
                    pool.wait_ge(demod_row[r], st.lap * (SLOTS // 2 * DMA) + ((j - 2) // 2 + 1) * DMA)
                    pool.wait_ge(s["cur_ready"], st.times(1, 2, 1))
                    for c in range(C):
                        nc.gpsimd.tensor_tensor(wo_b[:, c, :], wo_t[:, c, :], demod_o[:, r, :], ALU.mult).then_inc(s["wo_scaled"], 1)
                    for c in range(C):
                        pool.wait_ge(s["wo_scaled"], st.times(4, 2, c + 1))
                        style = cur[:, (j - 2) % SLOTS, 2 * C + c:2 * C + c + 1].to_broadcast([P, F])
                        last = nc.gpsimd.tensor_tensor(wo_b[:, c, :], wo_b[:, c, :], style, ALU.mult)
                    last.then_inc(s["wo_ready"], 1)
                if st.a:
                    pool.wait_ge(s["xt_ps"], st.times(4, 0, 4))
                    last = nc.gpsimd.tensor_tensor(xs[:, j, :, :], xs[:, j, :, :],
                                                   o_bias[:, :].unsqueeze(1).to_broadcast([P, G, F]), ALU.add)
                    last.then_inc(s["x_bias_ready"], 1)

            run_steps(pool, step)


def setup(nc, ctx, sb, s, x_v, cond_t, k_aff_t, k_aff_b, k_w_t, k_b, o_aff_t, o_aff_b, o_w_t, o_b, ident_in, mask_in,
          demod_dram, ident, mask, wk_t, wo_t, o_bias, k_bias, factors, xs, pt, vs, x_ready, ps_t, ps_p, ps_s):
    aff = sb("aff", [P, 2, SC, F])
    cond = sb("cond", [P, SC, B])
    aff_b = sb("aff_b", [P, 2, C])
    style_sq = sb("style_sq", [P, 2, C, B])
    w_sq = vs[:, :, :].rearrange("p u f -> p (u f)").rearrange("p (c f) -> p c f", c=C)
    var_k = sb("var_k", [P, C * B])
    inv_k = sb("inv_k", [P, C * B])
    tmp_k = sb("tmp_k", [P, C * B])
    var_o = sb("var_o", [B, F])
    inv_o = sb("inv_o", [B, F])
    tmp_o = sb("tmp_o", [B, F])

    with nc.Block() as block:
        @block.sync
        def _(sp):
            for src, dst in ((cond_t.rearrange("(c p) b -> p c b", p=P), cond[:, :, :]),
                             (k_aff_t.rearrange("(c p) i -> p c i", p=P), aff[:, 0, :, :]),
                             (o_aff_t.rearrange("(c p) i -> p c i", p=P), aff[:, 1, :, :]),
                             (k_aff_b, aff_b[:, 0, :]),
                             (o_aff_b, aff_b[:, 1, :]),
                             (k_b, k_bias[:, :]),
                             (k_w_t.rearrange("(c p) o -> p c o", p=P), wk_t[:, :, :]),
                             (o_w_t.rearrange("(c p) o -> p c o", p=P), wo_t[:, :, :]),
                             (ident_in, ident[:, :]),
                             (mask_in, mask[:, :]),
                             (o_b.partition_broadcast(P), o_bias[:, :])):
                sp.dma_start(dst, src).then_inc(s["loaded"], DMA)
            sp.dma_start(xs[:, 0, :, :], x_v[0]).then_inc(x_ready[0], DMA)
            sp.wait_ge(s["loaded"], 11 * DMA)
            sp.wait_ge(s["setup_dve"], 14)
            sp.dma_start(demod_dram, inv_o[:, :]).then_inc(s["demod_stored"], DMA)
            sp.wait_ge(s["demod_stored"], DMA)

        @block.tensor
        def _(pe):
            pe.wait_ge(s["loaded"], 11 * DMA)
            for m in range(2):
                for c in range(C):
                    for k in range(SC):
                        last = nc.tensor.matmul(ps_t[:, m, B * c:B * c + B], aff[:, m, k, P * c:P * c + P], cond[:, k, :],
                                                start=(k == 0), stop=(k == SC - 1))
                last.then_inc(s["setup_ps"], 1)
            pe.wait_ge(s["setup_dve"], 4)
            pe.wait_ge(s["setup_act"], 1)
            for c in range(C):
                for k in range(C):
                    last = nc.tensor.matmul(ps_p[:, 0, B * c:B * c + B], w_sq[:, k, P * c:P * c + P], style_sq[:, 0, k, :],
                                            start=(k == 0), stop=(k == C - 1))
            last.then_inc(s["setup_ps"], 1)
            pe.wait_ge(s["setup_act"], 2)
            for k in range(C):
                last = nc.tensor.matmul(ps_s[0:B, 0, :], style_sq[:, 1, k, :], w_sq[:, k, :],
                                        start=(k == 0), stop=(k == C - 1))
            last.then_inc(s["setup_ps"], 1)

        @block.scalar
        def _(act):
            act.wait_ge(s["loaded"], 11 * DMA)
            nc.scalar.activation(w_sq, wk_t[:, :, :], ACT.Square).then_inc(s["setup_act"], 1)
            act.wait_ge(s["setup_ps"], 3)
            nc.scalar.activation(w_sq, wo_t[:, :, :], ACT.Square).then_inc(s["setup_act"], 1)
            act.wait_ge(s["setup_dve"], 5)
            nc.scalar.activation(tmp_k[:, :], var_k[:, :], ACT.Sqrt).then_inc(s["setup_act"], 1)
            act.wait_ge(s["setup_dve"], 6)
            nc.scalar.activation(tmp_o[:, :], var_o[:, :], ACT.Sqrt).then_inc(s["setup_act"], 1)

        @block.vector
        def _(dve):
            done = [0]

            def link(ins):
                done[0] += 1
                ins.then_inc(s["setup_dve"], 1)
                dve.wait_ge(s["setup_dve"], done[0])

            dve.wait_ge(s["loaded"], 11 * DMA)
            for m in range(2):
                dve.wait_ge(s["setup_ps"], m + 1)
                style = factors[:, :, 2 * m * C:(2 * m + 1) * C].rearrange("p b c -> p c b")
                link(nc.vector.tensor_tensor(style, ps_t[:, m, 0:C * B].rearrange("p (c b) -> p c b", c=C),
                                             aff_b[:, m, :].unsqueeze(2).to_broadcast([P, C, B]), ALU.add))
                link(nc.vector.tensor_tensor(style_sq[:, m, :, :], style, style, ALU.mult))
            dve.wait_ge(s["setup_ps"], 3)
            link(nc.vector.tensor_scalar(var_k[:, :], ps_p[:, 0, 0:C * B], EPS, None, ALU.add))
            dve.wait_ge(s["setup_ps"], 4)
            link(nc.vector.tensor_scalar(var_o[:, :], ps_s[0:B, 0, :], EPS, None, ALU.add))
            for m, (var, inv, tmp) in enumerate(((var_k, inv_k, tmp_k), (var_o, inv_o, tmp_o))):
                dve.wait_ge(s["setup_act"], 3 + m)
                link(nc.vector.reciprocal(inv[:, :], tmp[:, :]))
                link(nc.vector.tensor_tensor(tmp[:, :], inv[:, :], inv[:, :], ALU.mult))
                link(nc.vector.scalar_tensor_tensor(out=tmp[:, :], in0=tmp[:, :], scalar=-0.5, in1=var[:, :],
                                                    op0=ALU.mult, op1=ALU.mult))
                link(nc.vector.scalar_tensor_tensor(out=inv[:, :], in0=tmp[:, :], scalar=1.5, in1=inv[:, :],
                                                    op0=ALU.add, op1=ALU.mult))
            link(nc.vector.tensor_copy(factors[:, :, C:2 * C].rearrange("p b c -> p c b"),
                                       inv_k[:, :].rearrange("p (c b) -> p c b", c=C)))

        @block.gpsimd
        def _(pool):
            nc.gpsimd.memset(pt[:, :, :, :], 0.0).then_inc(s["zeroed"], 1)
            pool.wait_ge(s["zeroed"], 1)


def kernel(x, cond_512, L0_cond_k_aff_w, L0_cond_k_aff_b, L0_cond_k_w, L0_cond_k_b,
           L0_cond_o_aff_w, L0_cond_o_aff_b, L0_cond_o_w, L0_cond_o_b):
    import numpy as np
    import concourse.bacc as bacc
    from concourse.bass_utils import run_bass_kernel_spmd

    def columns(v):
        return np.ascontiguousarray(np.asarray(v).reshape(C, P).T)

    token = np.arange(P)[:, None] % 32 // H
    arrays = {
        "x": np.ascontiguousarray(x),
        "cond_t": np.ascontiguousarray(np.asarray(cond_512).T),
        "k_aff_t": np.ascontiguousarray(np.asarray(L0_cond_k_aff_w).T),
        "k_aff_b": columns(L0_cond_k_aff_b),
        "k_w_t": np.ascontiguousarray(np.asarray(L0_cond_k_w).T),
        "k_b": columns(L0_cond_k_b),
        "o_aff_t": np.ascontiguousarray(np.asarray(L0_cond_o_aff_w).T),
        "o_aff_b": columns(L0_cond_o_aff_b),
        "o_w_t": np.ascontiguousarray(np.asarray(L0_cond_o_w).T),
        "o_b": np.ascontiguousarray(L0_cond_o_b),
        "ident": np.eye(P, dtype=np.float32),
        "mask": np.where(token == np.arange(32)[None, :] // H, 0.0, -1e30).astype(np.float32),
    }
    nc = bacc.Bacc("TRN2", target_bir_lowering=False, num_devices=1)
    args = [nc.dram_tensor(f"in_{name}", a.shape, F32, kind="ExternalInput").ap() for name, a in arrays.items()]
    out = nc.dram_tensor("out", (B, N, F), F32, kind="ExternalOutput").ap()
    demod_dram = nc.dram_tensor("demod_dram", (B, F), F32, kind="Internal").ap()
    build(nc, *args, out, demod_dram)
    got = run_bass_kernel_spmd(nc, [{f"in_{k}": a for k, a in arrays.items()}], core_ids=[0])
    return got.results[0]["out"]
```

```python
from contextlib import ExitStack

import concourse.bass as bass
from concourse import mybir
from concourse.alu_op_type import AluOpType as ALU

F32 = mybir.dt.float32
F32R = mybir.dt.float32r
ACT = mybir.ActivationFunctionType
AX_X = mybir.AxisListType.X

P = 128
B, N, F, S = 32, 512, 512, 256
H, D = 16, 32
C = F // P
HC = H // C
G = N // P
U = P // 8
Q = 4
SC = S // P
SLOTS = 4
SCALE = float(D) ** -0.5
EPS = 1e-8
DMA = 16


class Step:

    def __init__(self, lap, j, m=None):
        self.lap, self.j, self.m = lap, j, m
        self.t, self.k, self.sv, self.cd = (m is None or back <= m < B + back for back in range(4))

    def batch(self, back):
        return self.lap * SLOTS + (self.j - back)

    def times(self, per, back, more=0):
        return self.lap * (SLOTS * per) + (per * (self.j - back) + more)

    def first(self, steps):
        return self.m is not None and self.m < steps


def wait(eng, sem, value):
    if not isinstance(value, int) or value > 0:
        eng.wait_ge(sem, value)


def run_steps(eng, step):
    for m in range(SLOTS):
        step(Step(m // SLOTS, m % SLOTS, m))
    with eng.Fori(1, B // SLOTS) as lap:
        for j in range(SLOTS):
            step(Step(lap, j))
    for m in range(B, B + 3):
        step(Step(m // SLOTS, m % SLOTS, m))


def build(nc, x, cond_t, k_aff_t, k_aff_b, k_w_t, k_b, o_aff_t, o_aff_b, o_w_t, o_b, ident_in, mask_in, out, demod_dram):
    x_v = x.rearrange("b (g p) i -> b p g i", p=P)
    out_v = out.rearrange("b (g p) o -> b g p o", p=P)

    with ExitStack() as ctx:
        def sb(name, shape, dtype=F32):
            return ctx.enter_context(nc.sbuf_tensor(name, shape, dtype))

        ident = sb("ident", [P, P])
        mask = sb("mask", [P, 32])
        wk = sb("wk", [P, 2, C, F], F32R)
        wo = sb("wo", [P, 2, C, F], F32R)
        o_bias = sb("o_bias", [P, F])
        k_bias = sb("k_bias", [P, C])
        factors = sb("factors", [P, B, 3 * C])
        cur = sb("cur", [P, SLOTS, 3 * C])
        demod_o = sb("demod_o", [P, F])

        xs = sb("xs", [P, SLOTS, G, F])
        xt = sb("xt", [P, 2, C, N], F32R)
        ks = sb("ks", [P, C, N])
        kt_in = sb("kt_in", [P, H, P])
        kt = sb("kt", [P, P, H])
        vs = sb("vs", [P, U, P])
        sm = sb("sm", [P, 2, 512])
        pr = sb("pr", [P, 2, 512])
        mx = sb("mx", [P, 2, U])
        den = sb("den", [P, 2, U])
        rden = sb("rden", [P, 2, U])
        pq = sb("pq", [P, 2, 512])
        pt = sb("pt", [P, G, U, P])
        ot = sb("ot", [P, H, P])
        oc = sb("oc", [P, C, N])
        os_ = sb("os_", [P, 2, C, N], F32R)
        yo = sb("yo", [P, 2, F])

        names = """loaded demod_stored demod_row x_ready0 x_ready1 x_ready2 x_ready3 kt_landed
             oc_landed stored0 stored1 stored2 stored3
            setup_ps setup_dve setup_act split zeroed
            xt_ps k_ps v_ps s_ps av_ps o_ps
            cur_ready kt_ready xt_hi xt_lo ks_ready vs_ready exp_ready ot_ready os_hi os_lo
            s_read max_ready shifted sum_ready inv_ready prob_ready turned pt_ready yo_ready
            x_bias_ready out_ready""".split()
        s = {name: ctx.enter_context(nc.semaphore(name)) for name in names}
        x_ready = [s[f"x_ready{j}"] for j in range(SLOTS)]
        stored = [s[f"stored{j}"] for j in range(SLOTS)]

        def bank_pair(name):
            return ctx.enter_context(nc.psum_tensor(name, [P, 2, 512], F32))

        ps_t = bank_pair("ps_t")
        ps_p = bank_pair("ps_p")
        ps_s = bank_pair("ps_s")
        ps_a = bank_pair("ps_a")

        setup(nc, s, cond_t, k_aff_t, k_aff_b, k_w_t, k_b, o_aff_t, o_aff_b, o_w_t, o_b, ident_in, mask_in,
              demod_dram, ident, mask, wk, wo, o_bias, k_bias, factors, pt, vs, kt, ps_t, ps_p, ps_s)

        block = ctx.enter_context(nc.Block())

        @block.sync
        def _(sp):
            def early(value):
                if not isinstance(value, int):
                    sp.lower_val(value)
                return value

            def address(ap):
                early(ap.offset * 4)
                return ap

            def step(st):
                j = st.j
                if st.cd:
                    early(st.times(4, 3))
                    sp.wait_ge(s["ot_ready"], st.times(4, 3, 4))
                    wait(sp, s["os_hi"], st.times(4, 3))
                    wait(sp, s["os_lo"], st.times(4, 3))
                    for g in range(G):
                        for hh in range(HC):
                            sp.dma_start(oc[32 * hh:32 * hh + 32, :, P * g:P * g + P],
                                         ot[32 * g:32 * g + 32, hh:H:HC, :]).then_inc(s["oc_landed"], DMA)
                    row = address(demod_dram[st.batch(3), :].partition_broadcast(P))
                    wait(sp, s["yo_ready"], st.times(4, 3))
                    sp.dma_start(demod_o[:, :], row).then_inc(s["demod_row"], DMA)
                if st.t:
                    x_next = address(x_v[st.batch(0)])
                    if not st.first(SLOTS):
                        sp.wait_ge(stored[j], st.lap * (G * DMA))
                    sp.dma_start(xs[:, j, :, :], x_next).then_inc(x_ready[j], DMA)
                if st.k:
                    early(st.times(4, 1))
                    sp.wait_ge(s["ks_ready"], st.times(4, 1, 4))
                    wait(sp, s["kt_ready"], st.times(4, 1))
                    for hh in range(HC):
                        for g in range(G):
                            sp.dma_start(kt_in[32 * g:32 * g + 32, hh:H:HC, :],
                                         ks[32 * hh:32 * hh + 32, :, P * g:P * g + P]).then_inc(s["kt_landed"], DMA)
                if st.cd:
                    for g in range(G):
                        rows = address(out_v[st.batch(3), g])
                        sp.wait_ge(s["out_ready"], st.times(4, 3, g + 1))
                        sp.dma_start(rows, xs[:, (j - 3) % SLOTS, g, :]).then_inc(stored[(j - 3) % SLOTS], DMA)

            run_steps(sp, step)
            for j in range(SLOTS):
                sp.wait_ge(stored[j], (B // SLOTS) * G * DMA)

        @block.tensor
        def _(pe):
            def attention_out(st, k):
                if k == 0:
                    pe.wait_ge(s["vs_ready"], st.times(4, 3, 4))
                    pe.wait_ge(s["pt_ready"], st.times(4, 3, 4))
                wait(pe, s["ot_ready"], st.times(4, 3, k - 1))
                for ul in range(4):
                    for g in range(G):
                        u = 4 * k + ul
                        last = nc.tensor.matmul(ps_a[32 * g:32 * g + 32, k % 2, P * ul:P * ul + P],
                                                vs[:, u, 32 * g:32 * g + 32], pt[:, g, u, :],
                                                start=True, stop=True)
                last.then_inc(s["av_ps"], 1)

            def v_rows(st, k):
                if k < 2 and (st.m is None or st.m <= B):
                    wait(pe, s["xt_lo"], st.times(4, 1, 3 + k))
                else:
                    wait(pe, s["vs_ready"], st.times(4, 2, k - 1))
                for ul in range(4):
                    u = 4 * k + ul
                    last = nc.tensor.transpose(ps_t[:, k % 2, P * ul:P * ul + P],
                                               kt[:, 8 * u:8 * u + 8, :].rearrange("p t h -> p (t h)"), ident[:, :])
                last.then_inc(s["v_ps"], 1)

            def scores_wait(st, g):
                if g == 0:
                    pe.wait_ge(s["kt_ready"], st.times(4, 2, 4))
                wait(pe, s["s_read"], st.times(4, 2, g - 1))

            def scores(st, g):
                for u in range(U):
                    for q in range(Q):
                        t = 8 * u + 2 * q
                        rows = kt[32 * g:32 * g + 32, t:t + 2, :].rearrange("p t h -> p (t h)")
                        last = nc.tensor.matmul(ps_s[32 * q:32 * q + 32, g % 2, 32 * u:32 * u + 32], rows, rows,
                                                start=True, stop=True)
                last.then_inc(s["s_ps"], 1)

            def x_transposes(st, c):
                if c == 0:
                    pe.wait_ge(x_ready[st.j], (st.lap + 1) * DMA)
                if c >= 2:
                    pe.wait_ge(s["xt_lo"], st.times(4, 0, c - 1))
                elif st.sv:
                    pe.wait_ge(s["vs_ready"], st.times(4, 2, 3 + c))
                else:
                    wait(pe, s["xt_lo"], st.times(4, 1, 3 + c))
                for g in range(G):
                    last = nc.tensor.transpose(ps_t[:, c % 2, P * g:P * g + P],
                                               xs[:, st.j, g, P * c:P * c + P], ident[:, :])
                last.then_inc(s["xt_ps"], 1)

            def product(bank, weight, w_cols, data, d_cols, weight_stationary, split_until=None):
                terms = [(a, b, i) for i in range(C) for a, b in ((0, 0), (0, 1), (1, 0))]
                for n, (a, b, i) in enumerate(terms):
                    w, d = weight[:, a, i, w_cols], data[:, b, i, d_cols]
                    if split_until and n % 3 == 0:
                        lo_ready, count = split_until
                        pe.wait_ge(lo_ready, count(i + 1))
                    stationary, moving = (w, d) if weight_stationary else (d, w)
                    last = nc.tensor.matmul(bank, stationary, moving, start=(n == 0), stop=(n == len(terms) - 1))
                return last

            def k_projection(st, c):
                if c >= 2:
                    pe.wait_ge(s["ks_ready"], st.times(4, 1, c - 1))
                elif st.first(4):
                    wait(pe, s["ks_ready"], st.times(4, 2, 3 + c))
                else:
                    pe.wait_ge(s["yo_ready"], st.times(4, 4, 3 + c))
                product(ps_p[:, c % 2, :], wk, slice(P * c, P * c + P), xt, slice(0, N), True,
                        (s["xt_lo"], lambda n: st.times(4, 1, n)) if c == 0 else None).then_inc(s["k_ps"], 1)

            def o_projection(st, g):
                if g < 2 and st.k:
                    pe.wait_ge(s["ks_ready"], st.times(4, 1, 3 + g))
                else:
                    wait(pe, s["yo_ready"], st.times(4, 3, g - 1))
                product(ps_p[:, g % 2, :], wo, slice(0, F), os_, slice(P * g, P * g + P), False,
                        (s["os_lo"], lambda n: st.times(4, 3, n)) if g == 0 else None).then_inc(s["o_ps"], 1)

            def step(st):
                if st.k:
                    k_projection(st, 0)
                if st.cd:
                    for k in range(4):
                        if st.sv and k == 3:
                            scores_wait(st, 0)
                        attention_out(st, k)
                elif st.sv:
                    scores_wait(st, 0)
                for g in range(4):
                    if st.sv:
                        scores(st, g)
                        if g < G - 1:
                            scores_wait(st, g + 1)
                        v_rows(st, g)
                    if st.k and g < C - 1:
                        k_projection(st, g + 1)
                for g in range(4):
                    if st.cd:
                        o_projection(st, g)
                    if st.t:
                        x_transposes(st, g)

            run_steps(pe, step)

        @block.scalar
        def _(act):
            def kt_rows(st, k):
                if k == 0:
                    act.wait_ge(s["kt_landed"], st.times(H * DMA, 2, H * DMA))
                    wait(act, s["s_ps"], st.times(4, 2))
                    wait(act, s["v_ps"], st.times(4, 2))
                nc.scalar.activation(kt[:, 32 * k:32 * k + 32, :],
                                     kt_in[:, :, 32 * k:32 * k + 32].rearrange("p h t -> p t h"),
                                     ACT.Copy).then_inc(s["kt_ready"], 1)

            def out_columns(st, k):
                if k == 0:
                    wait(act, s["oc_landed"], st.times(H * DMA, 3))
                act.wait_ge(s["av_ps"], st.times(4, 3, k + 1))
                nc.scalar.activation(ot[:, :, 32 * k:32 * k + 32],
                                     ps_a[:, k % 2, :].rearrange("p (t h) -> p h t", h=H),
                                     ACT.Copy).then_inc(s["ot_ready"], 1)

            def v_out(st, k):
                if k == 0:
                    wait(act, s["av_ps"], st.times(4, 2))
                act.wait_ge(s["v_ps"], st.times(4, 2, k + 1))
                nc.scalar.activation(vs[:, 4 * k:4 * k + 4, :], ps_t[:, k % 2, :].rearrange("p (u f) -> p u f", u=4),
                                     ACT.Copy).then_inc(s["vs_ready"], 1)

            def exps(st, g):
                act.wait_ge(s["shifted"], st.times(4, 2, g + 1))
                wait(act, s["turned"], st.times(4, 2, g - 1))
                nc.scalar.activation(pr[:, g % 2, :], sm[:, g % 2, :], ACT.Exp, scale=SCALE).then_inc(s["exp_ready"], 1)

            def spread(st, g):
                if g == 0:
                    wait(act, s["av_ps"], st.times(4, 2))
                act.wait_ge(s["turned"], st.times(4, 2, g + 1))
                for q in range(Q):
                    rows = slice(32 * q, 32 * q + 32)
                    last = nc.scalar.activation(pt[rows, g, :, 32 * q:32 * q + 32],
                                                pq[rows, g % 2, :].rearrange("p (u f) -> p u f", u=U), ACT.Copy)
                last.then_inc(s["pt_ready"], 1)

            def k_out(st, c):
                if c == 0:
                    wait(act, s["kt_landed"], st.times(H * DMA, 1))
                act.wait_ge(s["k_ps"], st.times(4, 1, c + 1))
                slot = (st.j - 1) % SLOTS
                nc.scalar.activation(ks[:, c, :], ps_p[:, c % 2, :], ACT.Identity, bias=k_bias[:, c:c + 1],
                                     scale=cur[:, slot, C + c:C + c + 1]).then_inc(s["ks_ready"], 1)

            def os_high(st, c):
                if c == 0:
                    act.wait_ge(s["oc_landed"], st.times(H * DMA, 3, H * DMA))
                    wait(act, s["o_ps"], st.times(4, 3))
                slot = (st.j - 3) % SLOTS
                nc.scalar.activation(os_[:, 0, c, :], oc[:, c, :], ACT.Copy,
                                     scale=cur[:, slot, 2 * C + c:2 * C + c + 1]).then_inc(s["os_hi"], 1)

            def x_high(st, c):
                if c == 0:
                    act.wait_ge(s["cur_ready"], st.times(1, 0, 1))
                    wait(act, s["k_ps"], st.times(4, 0))
                act.wait_ge(s["xt_ps"], st.times(4, 0, c + 1))
                nc.scalar.activation(xt[:, 0, c, :], ps_t[:, c % 2, :], ACT.Copy,
                                     scale=cur[:, st.j, c:c + 1]).then_inc(s["xt_hi"], 1)

            def step(st):
                if st.t:
                    wait(act, s["os_lo"], st.times(4, 3))
                    nc.scalar.activation(cur[:, st.j, :], factors[:, st.batch(0), :], ACT.Copy).then_inc(s["cur_ready"], 1)
                if st.sv:
                    kt_rows(st, 0)
                for k in range(4):
                    if st.sv and k < 3:
                        kt_rows(st, k + 1)
                for k in range(4):
                    if st.cd:
                        out_columns(st, k)
                if st.k:
                    k_out(st, 0)
                for g in range(4):
                    if st.sv:
                        v_out(st, g)
                        exps(st, g)
                    if st.cd and g == 2:
                        for c in range(C):
                            os_high(st, c)
                    if st.k and g < C - 1:
                        k_out(st, g + 1)
                    if st.sv and 0 < g < 3:
                        spread(st, g - 1)
                if st.t:
                    x_high(st, 0)
                if st.sv:
                    spread(st, 2)
                if st.t:
                    x_high(st, 1)
                    x_high(st, 2)
                if st.sv:
                    spread(st, 3)
                if st.t:
                    x_high(st, 3)

            run_steps(act, step)

        @block.vector
        def _(dve):
            def scores_in(st, g):
                r = g % 2
                blocks = sm[:, r, :].rearrange("p (u f) -> p u f", u=U)
                dve.wait_ge(s["s_ps"], st.times(4, 2, g + 1))
                wait(dve, s["exp_ready"], st.times(4, 2, g - 1))
                nc.vector.tensor_tensor(blocks, ps_s[:, r, :].rearrange("p (u f) -> p u f", u=U),
                                        mask[:, :].unsqueeze(1).to_broadcast([P, U, 32]), ALU.add).then_inc(s["s_read"], 1)
                dve.wait_ge(s["s_read"], st.times(4, 2, g + 1))
                nc.vector.tensor_reduce(mx[:, r, :], blocks, AX_X, ALU.max).then_inc(s["max_ready"], 1)

            def probabilities(st, g):
                r = g % 2
                blocks = pr[:, r, :].rearrange("p (u f) -> p u f", u=U)
                dve.wait_ge(s["exp_ready"], st.times(4, 2, g + 1))
                nc.vector.tensor_reduce(den[:, r, :], blocks, AX_X, ALU.add).then_inc(s["sum_ready"], 1)
                dve.wait_ge(s["sum_ready"], st.times(4, 2, g + 1))
                nc.vector.reciprocal(rden[:, r, :], den[:, r, :]).then_inc(s["inv_ready"], 1)
                dve.wait_ge(s["inv_ready"], st.times(4, 2, g + 1))
                nc.vector.tensor_tensor(blocks, blocks, rden[:, r, :].unsqueeze(2).to_broadcast([P, U, 32]),
                                        ALU.mult).then_inc(s["prob_ready"], 1)
                dve.wait_ge(s["prob_ready"], st.times(4, 2, g + 1))
                wait(dve, s["pt_ready"], st.times(4, 2, g - 1))
                nc.vector.transpose(pq[:, r, :], pr[:, r, :]).then_inc(s["turned"], 1)

            def os_low(st, c):
                slot = (st.j - 3) % SLOTS
                dve.wait_ge(s["os_hi"], st.times(4, 3, c + 1))
                nc.vector.scalar_tensor_tensor(
                    out=os_[:, 1, c, :], in0=oc[:, c, :], scalar=cur[:, slot, 2 * C + c:2 * C + c + 1],
                    in1=os_[:, 0, c, :].bitcast(F32), op0=ALU.mult, op1=ALU.subtract).then_inc(s["os_lo"], 1)

            def demodulated(st, g):
                if g == 0:
                    dve.wait_ge(s["demod_row"], st.times(DMA, 3, DMA))
                wait(dve, s["out_ready"], st.times(4, 3, g - 1))
                dve.wait_ge(s["o_ps"], st.times(4, 3, g + 1))
                nc.vector.tensor_tensor(yo[:, g % 2, :], ps_p[:, g % 2, :], demod_o[:, :], ALU.mult).then_inc(s["yo_ready"], 1)

            def x_low(st, c):
                dve.wait_ge(s["xt_hi"], st.times(4, 0, c + 1))
                nc.vector.scalar_tensor_tensor(out=xt[:, 1, c, :], in0=ps_t[:, c % 2, :], scalar=cur[:, st.j, c:c + 1],
                                               in1=xt[:, 0, c, :].bitcast(F32), op0=ALU.mult,
                                               op1=ALU.subtract).then_inc(s["xt_lo"], 1)

            def step(st):
                if st.sv:
                    scores_in(st, 0)
                    scores_in(st, 1)
                    probabilities(st, 0)
                    scores_in(st, 2)
                    probabilities(st, 1)
                if st.cd:
                    for c in range(C):
                        os_low(st, c)
                if st.sv:
                    scores_in(st, 3)
                    probabilities(st, 2)
                if st.cd:
                    demodulated(st, 0)
                if st.t:
                    x_low(st, 0)
                if st.cd:
                    demodulated(st, 1)
                if st.sv:
                    probabilities(st, 3)
                if st.t:
                    x_low(st, 1)
                if st.cd:
                    demodulated(st, 2)
                if st.t:
                    x_low(st, 2)
                    x_low(st, 3)
                if st.cd:
                    demodulated(st, 3)

            run_steps(dve, step)

        @block.gpsimd
        def _(pool):
            def shift(st, g):
                r = g % 2
                blocks = sm[:, r, :].rearrange("p (u f) -> p u f", u=U)
                pool.wait_ge(s["max_ready"], st.times(4, 2, g + 1))
                nc.gpsimd.tensor_tensor(blocks, blocks, mx[:, r, :].unsqueeze(2).to_broadcast([P, U, 32]),
                                        ALU.subtract).then_inc(s["shifted"], 1)

            def step(st):
                if st.sv:
                    for g in range(G):
                        shift(st, g)
                if st.cd:
                    for g in range(G):
                        if g == 0:
                            pool.wait_ge(s["x_bias_ready"], st.times(1, 3, 1))
                        pool.wait_ge(s["yo_ready"], st.times(4, 3, g + 1))
                        rows = xs[:, (st.j - 3) % SLOTS, g, :]
                        nc.gpsimd.tensor_tensor(rows, rows, yo[:, g % 2, :], ALU.add).then_inc(s["out_ready"], 1)
                if st.t:
                    pool.wait_ge(s["xt_ps"], st.times(4, 0, 4))
                    rows = xs[:, st.j, :, :]
                    nc.gpsimd.tensor_tensor(rows, rows, o_bias[:, :].unsqueeze(1).to_broadcast([P, G, F]),
                                            ALU.add).then_inc(s["x_bias_ready"], 1)

            run_steps(pool, step)


def setup(nc, s, cond_t, k_aff_t, k_aff_b, k_w_t, k_b, o_aff_t, o_aff_b, o_w_t, o_b, ident_in, mask_in,
          demod_dram, ident, mask, wk, wo, o_bias, k_bias, factors, pt, vs, kt, ps_t, ps_p, ps_s):
    flat = pt[:, :, :, :].rearrange("p g u f -> p (g u f)")
    wk_t, wo_t, w_sq, aff = (flat[:, 2048 * n:2048 * n + 2048] for n in range(4))
    wk_t, wo_t, w_sq = (v.rearrange("p (c f) -> p c f", c=C) for v in (wk_t, wo_t, w_sq))
    aff = aff.rearrange("p (m k f) -> p m k f", m=2, k=SC)
    rows = vs[0:B, :, :].rearrange("p u f -> p (u f)")
    var_o, inv_o, tmp_o = (rows[:, F * n:F * n + F] for n in range(3))
    small = kt[:, :, :].rearrange("p t h -> p (t h)")
    var_k, inv_k, tmp_k = (small[:, C * B * n:C * B * n + C * B] for n in range(3))
    style_sq = small[:, 512:512 + 2 * C * B].rearrange("p (m c b) -> p m c b", m=2, c=C)
    cond = small[:, 1024:1024 + SC * B].rearrange("p (c b) -> p c b", c=SC)
    aff_b = small[:, 1536:1536 + 2 * C].rearrange("p (m c) -> p m c", m=2)

    with nc.Block() as block:
        @block.sync
        def _(sp):
            for src, dst in ((cond_t.rearrange("(c p) b -> p c b", p=P), cond),
                             (k_aff_t.rearrange("(c p) i -> p c i", p=P), aff[:, 0, :, :]),
                             (o_aff_t.rearrange("(c p) i -> p c i", p=P), aff[:, 1, :, :]),
                             (k_aff_b, aff_b[:, 0, :]),
                             (o_aff_b, aff_b[:, 1, :]),
                             (k_b, k_bias[:, :]),
                             (k_w_t.rearrange("(c p) o -> p c o", p=P), wk_t),
                             (o_w_t.rearrange("(c p) o -> p c o", p=P), wo_t),
                             (ident_in, ident[:, :]),
                             (mask_in, mask[:, :]),
                             (o_b.partition_broadcast(P), o_bias[:, :])):
                sp.dma_start(dst, src).then_inc(s["loaded"], DMA)
            sp.wait_ge(s["setup_dve"], 14)
            sp.dma_start(demod_dram, inv_o).then_inc(s["demod_stored"], DMA)
            sp.wait_ge(s["demod_stored"], DMA)

        @block.tensor
        def _(pe):
            pe.wait_ge(s["loaded"], 11 * DMA)
            for m in range(2):
                for c in range(C):
                    for k in range(SC):
                        last = nc.tensor.matmul(ps_t[:, m, B * c:B * c + B], aff[:, m, k, P * c:P * c + P], cond[:, k, :],
                                                start=(k == 0), stop=(k == SC - 1))
                last.then_inc(s["setup_ps"], 1)
            pe.wait_ge(s["setup_dve"], 4)
            pe.wait_ge(s["setup_act"], 1)
            for c in range(C):
                for k in range(C):
                    last = nc.tensor.matmul(ps_p[:, 0, B * c:B * c + B], w_sq[:, k, P * c:P * c + P], style_sq[:, 0, k, :],
                                            start=(k == 0), stop=(k == C - 1))
            last.then_inc(s["setup_ps"], 1)
            pe.wait_ge(s["setup_act"], 2)
            for k in range(C):
                last = nc.tensor.matmul(ps_s[0:B, 0, :], style_sq[:, 1, k, :], w_sq[:, k, :],
                                        start=(k == 0), stop=(k == C - 1))
            last.then_inc(s["setup_ps"], 1)

        @block.scalar
        def _(act):
            act.wait_ge(s["loaded"], 11 * DMA)
            nc.scalar.activation(w_sq, wk_t, ACT.Square).then_inc(s["setup_act"], 1)
            nc.scalar.activation(wk[:, 0, :, :], wk_t, ACT.Copy).then_inc(s["split"], 1)
            nc.scalar.activation(wo[:, 0, :, :], wo_t, ACT.Copy).then_inc(s["split"], 1)
            act.wait_ge(s["setup_ps"], 3)
            nc.scalar.activation(w_sq, wo_t, ACT.Square).then_inc(s["setup_act"], 1)
            act.wait_ge(s["setup_dve"], 5)
            nc.scalar.activation(tmp_k, var_k, ACT.Sqrt).then_inc(s["setup_act"], 1)
            act.wait_ge(s["setup_dve"], 6)
            nc.scalar.activation(tmp_o, var_o, ACT.Sqrt).then_inc(s["setup_act"], 1)
            act.wait_ge(s["zeroed"], 1)

        @block.vector
        def _(dve):
            done = [0]

            def link(ins):
                done[0] += 1
                ins.then_inc(s["setup_dve"], 1)
                dve.wait_ge(s["setup_dve"], done[0])

            dve.wait_ge(s["loaded"], 11 * DMA)
            for m in range(2):
                dve.wait_ge(s["setup_ps"], m + 1)
                style = factors[:, :, 2 * m * C:(2 * m + 1) * C].rearrange("p b c -> p c b")
                link(nc.vector.tensor_tensor(style, ps_t[:, m, 0:C * B].rearrange("p (c b) -> p c b", c=C),
                                             aff_b[:, m, :].unsqueeze(2).to_broadcast([P, C, B]), ALU.add))
                link(nc.vector.tensor_tensor(style_sq[:, m, :, :], style, style, ALU.mult))
            dve.wait_ge(s["setup_ps"], 3)
            link(nc.vector.tensor_scalar(var_k, ps_p[:, 0, 0:C * B], EPS, None, ALU.add))
            dve.wait_ge(s["setup_ps"], 4)
            link(nc.vector.tensor_scalar(var_o, ps_s[0:B, 0, :], EPS, None, ALU.add))
            for m, (var, inv, tmp) in enumerate(((var_k, inv_k, tmp_k), (var_o, inv_o, tmp_o))):
                dve.wait_ge(s["setup_act"], 3 + m)
                link(nc.vector.reciprocal(inv, tmp))
                link(nc.vector.tensor_tensor(tmp, inv, inv, ALU.mult))
                link(nc.vector.scalar_tensor_tensor(out=tmp, in0=tmp, scalar=-0.5, in1=var,
                                                    op0=ALU.mult, op1=ALU.mult))
                link(nc.vector.scalar_tensor_tensor(out=inv, in0=tmp, scalar=1.5, in1=inv,
                                                    op0=ALU.add, op1=ALU.mult))
            link(nc.vector.tensor_copy(factors[:, :, C:2 * C].rearrange("p b c -> p c b"),
                                       inv_k.rearrange("p (c b) -> p c b", c=C)))
            dve.wait_ge(s["split"], 2)
            link(nc.vector.tensor_tensor(wk[:, 1, :, :], wk_t, wk[:, 0, :, :].bitcast(F32), ALU.subtract))
            link(nc.vector.tensor_tensor(wo[:, 1, :, :], wo_t, wo[:, 0, :, :].bitcast(F32), ALU.subtract))
            nc.vector.memset(pt[:, :, :, :], 0.0).then_inc(s["zeroed"], 1)
            dve.wait_ge(s["zeroed"], 1)


def kernel(x, cond_512, L0_cond_k_aff_w, L0_cond_k_aff_b, L0_cond_k_w, L0_cond_k_b,
           L0_cond_o_aff_w, L0_cond_o_aff_b, L0_cond_o_w, L0_cond_o_b):
    import numpy as np
    import concourse.bacc as bacc
    from concourse.bass_utils import run_bass_kernel_spmd

    def columns(v):
        return np.ascontiguousarray(np.asarray(v).reshape(C, P).T)

    token = np.arange(P)[:, None] % 32 // H
    arrays = {
        "x": np.ascontiguousarray(x),
        "cond_t": np.ascontiguousarray(np.asarray(cond_512).T),
        "k_aff_t": np.ascontiguousarray(np.asarray(L0_cond_k_aff_w).T),
        "k_aff_b": columns(L0_cond_k_aff_b),
        "k_w_t": np.ascontiguousarray(np.asarray(L0_cond_k_w).T),
        "k_b": columns(L0_cond_k_b),
        "o_aff_t": np.ascontiguousarray(np.asarray(L0_cond_o_aff_w).T),
        "o_aff_b": columns(L0_cond_o_aff_b),
        "o_w_t": np.ascontiguousarray(np.asarray(L0_cond_o_w).T),
        "o_b": np.ascontiguousarray(L0_cond_o_b),
        "ident": np.eye(P, dtype=np.float32),
        "mask": np.where(token == np.arange(32)[None, :] // H, 0.0, -1e30).astype(np.float32),
    }
    nc = bacc.Bacc("TRN2", target_bir_lowering=False, num_devices=1)
    args = [nc.dram_tensor(f"in_{name}", a.shape, F32, kind="ExternalInput").ap() for name, a in arrays.items()]
    out = nc.dram_tensor("out", (B, N, F), F32, kind="ExternalOutput").ap()
    demod_dram = nc.dram_tensor("demod_dram", (B, F), F32, kind="Internal").ap()
    build(nc, *args, out, demod_dram)
    got = run_bass_kernel_spmd(nc, [{f"in_{k}": a for k, a in arrays.items()}], core_ids=[0])
    return got.results[0]["out"]
```

```python
from contextlib import ExitStack

import concourse.bass as bass
from concourse import mybir
from concourse.alu_op_type import AluOpType as ALU

F32 = mybir.dt.float32
F32R = mybir.dt.float32r
ACT = mybir.ActivationFunctionType
AX_X = mybir.AxisListType.X

P = 128
B, N, F, S = 32, 512, 512, 256
H, D = 16, 32
C = F // P
HC = H // C
G = N // P
U = P // 8
Q = 4
SC = S // P
SLOTS = 4
SCALE = float(D) ** -0.5
EPS = 1e-8
DMA = 16


class Step:

    def __init__(self, lap, j, m=None):
        self.lap, self.j, self.m = lap, j, m
        self.last = m == B + 2
        self.k_first = m == 2
        self.t, self.k, self.sv, self.cd = (m is None or back <= m < B + back for back in range(4))

    def batch(self, back):
        return self.lap * SLOTS + (self.j - back)

    def times(self, per, back, more=0):
        return self.lap * (SLOTS * per) + (per * (self.j - back) + more)

    def first(self, steps):
        return self.m is not None and self.m < steps


def wait(eng, sem, value):
    if not isinstance(value, int) or value > 0:
        eng.wait_ge(sem, value)


def run_steps(eng, step, setup):
    for m in range(SLOTS):
        if m < len(setup):
            setup[m]()
        step(Step(m // SLOTS, m % SLOTS, m))
    with eng.Fori(1, B // SLOTS) as lap:
        for j in range(SLOTS):
            step(Step(lap, j))
    for m in range(B, B + 3):
        step(Step(m // SLOTS, m % SLOTS, m))


def build(nc, x, cond_t, k_aff_t, k_aff_b, k_w_t, k_b, o_aff_t, o_aff_b, o_w_t, o_b, ident_in, mask_in, out, demod_dram):
    x_v = x.rearrange("b (g p) i -> b p g i", p=P)
    out_v = out.rearrange("b (g p) o -> b g p o", p=P)

    with ExitStack() as ctx:
        def sb(name, shape, dtype=F32):
            return ctx.enter_context(nc.sbuf_tensor(name, shape, dtype))

        ident = sb("ident", [P, P])
        mask = sb("mask", [P, 32])
        wk = sb("wk", [P, 2, C, F], F32R)
        wo = sb("wo", [P, 2, C, F], F32R)
        o_bias = sb("o_bias", [P, F])
        k_bias = sb("k_bias", [P, C])
        factors = sb("factors", [P, B, 3 * C])
        cur = sb("cur", [P, SLOTS, 3 * C])
        demod_o = sb("demod_o", [P, F])

        xs = sb("xs", [P, SLOTS, G, F])
        xt = sb("xt", [P, 2, C, N], F32R)
        ks = sb("ks", [P, C, N])
        kt_in = sb("kt_in", [P, H, P])
        kt = sb("kt", [P, P, H])
        vs = sb("vs", [P, U, P])
        sm = sb("sm", [P, 2, 512])
        pr = sb("pr", [P, 2, 512])
        mx = sb("mx", [P, 2, U])
        den = sb("den", [P, 2, U])
        rden = sb("rden", [P, 2, U])
        pq = sb("pq", [P, 2, 512])
        pt = sb("pt", [P, G, U, P])
        ot = sb("ot", [P, H, P])
        oc = sb("oc", [P, C, N])
        os_ = sb("os_", [P, 2, C, N], F32R)
        yo = sb("yo", [P, 2, F])

        names = """
            style_loaded ident_loaded wk_loaded consts_loaded wo_loaded demod_stored demod_row
            x_ready0 x_ready1 x_ready2 x_ready3 kt_landed oc_landed oc_group0 oc_group1 oc_group2 oc_group3
            stored0 stored1 stored2 stored3
            style_k_ps var_k_ps style_o_ps var_o_ps xt_ps k_ps v_ps s_ps av_ps o_ps
            wk_squared wo_squared wk_hi wo_hi root_k root_o cur_style_k cur_demod_k cur_style_o
            kt_ready xt_hi ks_ready vs_ready exp_ready pt_ready ot_ready os_hi
            factors_k factors_o wk_lo wo_lo xt_lo os_lo s_read max_ready sum_ready inv_ready prob_ready turned yo_ready
            zeroed shifted x_bias_ready out_ready""".split()
        s = {name: ctx.enter_context(nc.semaphore(name)) for name in names}
        x_ready = [s[f"x_ready{j}"] for j in range(SLOTS)]
        group_landed = [s[f"oc_group{g}"] for g in range(G)]
        stored = [s[f"stored{j}"] for j in range(SLOTS)]

        def bank_pair(name):
            return ctx.enter_context(nc.psum_tensor(name, [P, 2, 512], F32))

        ps_t = bank_pair("ps_t")
        ps_p = bank_pair("ps_p")
        ps_s = bank_pair("ps_s")
        ps_a = bank_pair("ps_a")

        stage_k = pt[:, :, :, :].rearrange("p g u f -> p (g u f)")
        wk_t = stage_k[:, 0:C * F].rearrange("p (c f) -> p c f", c=C)
        wk_sq = stage_k[:, C * F:2 * C * F].rearrange("p (c f) -> p c f", c=C)
        aff_k = stage_k[:, 2 * C * F:(2 * C + SC) * F].rearrange("p (k f) -> p k f", k=SC)
        wo_t = oc
        wo_sq = ot[:, :, :].rearrange("p h t -> p (h t)").rearrange("p (c f) -> p c f", c=C)
        aff_o = vs[:, :, :].rearrange("p u f -> p (u f)")[:, 0:SC * F].rearrange("p (k f) -> p k f", k=SC)
        var_o, tmp_o, inv_o = pr[0:B, 0, :], pr[0:B, 1, :], demod_o[0:B, :]
        small = yo[:, :, :].rearrange("p a f -> p (a f)")
        var_k, inv_k, tmp_k = (small[:, C * B * n:C * B * n + C * B] for n in range(3))
        style_sq = small[:, 3 * C * B:5 * C * B].rearrange("p (m c b) -> p m c b", m=2, c=C)
        cond = small[:, 5 * C * B:(5 * C + SC) * B].rearrange("p (c b) -> p c b", c=SC)
        aff_b = small[:, (5 * C + SC) * B:(5 * C + SC) * B + 2 * C].rearrange("p (m c) -> p m c", m=2)

        block = ctx.enter_context(nc.Block())

        @block.sync
        def _(sp):
            def early(value):
                if not isinstance(value, int):
                    sp.lower_val(value)
                return value

            def address(ap):
                early(ap.offset * 4)
                return ap

            def step(st):
                j = st.j
                if st.cd:
                    early(st.times(4, 3))
                    sp.wait_ge(s["ot_ready"], st.times(4, 3, 4))
                    wait(sp, s["os_hi"], st.times(4, 3))
                    wait(sp, s["os_lo"], st.times(4, 3))
                    for g in range(G):
                        landed = group_landed[g] if st.last else s["oc_landed"]
                        for hh in range(HC):
                            sp.dma_start(oc[32 * hh:32 * hh + 32, :, P * g:P * g + P],
                                         ot[32 * g:32 * g + 32, hh:H:HC, :]).then_inc(landed, DMA)
                    row = address(demod_dram[st.batch(3), :].partition_broadcast(P))
                    wait(sp, s["yo_ready"], st.times(4, 3))
                    sp.dma_start(demod_o[:, :], row).then_inc(s["demod_row"], DMA)
                if st.t:
                    x_next = address(x_v[st.batch(0)])
                    if not st.first(SLOTS):
                        sp.wait_ge(stored[j], st.lap * (G * DMA))
                    sp.dma_start(xs[:, j, :, :], x_next).then_inc(x_ready[j], DMA)
                if st.k:
                    early(st.times(4, 1))
                    sp.wait_ge(s["ks_ready"], st.times(4, 1, 4))
                    wait(sp, s["kt_ready"], st.times(4, 1))
                    for hh in range(HC):
                        for g in range(G):
                            sp.dma_start(kt_in[32 * g:32 * g + 32, hh:H:HC, :],
                                         ks[32 * hh:32 * hh + 32, :, P * g:P * g + P]).then_inc(s["kt_landed"], DMA)
                if st.cd:
                    for g in range(G):
                        rows = address(out_v[st.batch(3), g])
                        sp.wait_ge(s["out_ready"], st.times(4, 3, g + 1))
                        sp.dma_start(rows, xs[:, (j - 3) % SLOTS, g, :]).then_inc(stored[(j - 3) % SLOTS], DMA)

            def load(pairs, sem):
                for src, dst in pairs:
                    sp.dma_start(dst, src).then_inc(s[sem], DMA)

            def setup_styles():
                load(((cond_t.rearrange("(c p) b -> p c b", p=P), cond),
                      (k_aff_t.rearrange("(c p) i -> p c i", p=P), aff_k),
                      (k_aff_b, aff_b[:, 0, :])), "style_loaded")
                load(((ident_in, ident[:, :]),), "ident_loaded")

            def setup_weights():
                load(((k_w_t.rearrange("(c p) o -> p c o", p=P), wk_t),
                      (k_b, k_bias[:, :])), "wk_loaded")
                load(((mask_in, mask[:, :]),
                      (o_b.partition_broadcast(P), o_bias[:, :])), "consts_loaded")
                load(((o_w_t.rearrange("(c p) o -> p c o", p=P), wo_t[:, :, :]),
                      (o_aff_t.rearrange("(c p) i -> p c i", p=P), aff_o),
                      (o_aff_b, aff_b[:, 1, :])), "wo_loaded")

            def store_demod():
                sp.wait_ge(s["factors_o"], 7)
                sp.dma_start(demod_dram, inv_o).then_inc(s["demod_stored"], DMA)
                sp.wait_ge(s["demod_stored"], DMA)

            run_steps(sp, step, [setup_styles, setup_weights, store_demod])
            for j in range(SLOTS):
                sp.wait_ge(stored[j], (B // SLOTS) * G * DMA)

        @block.tensor
        def _(pe):
            def attention_out(st, k):
                if k == 0:
                    pe.wait_ge(s["vs_ready"], st.times(4, 3, 4))
                    pe.wait_ge(s["pt_ready"], st.times(4, 3, 4))
                wait(pe, s["ot_ready"], st.times(4, 3, k - 1))
                for ul in range(4):
                    for g in range(G):
                        u = 4 * k + ul
                        last = nc.tensor.matmul(ps_a[32 * g:32 * g + 32, k % 2, P * ul:P * ul + P],
                                                vs[:, u, 32 * g:32 * g + 32], pt[:, g, u, :],
                                                start=True, stop=True)
                last.then_inc(s["av_ps"], 1)

            def v_rows(st, k):
                if k < 2 and (st.m is None or st.m <= B):
                    wait(pe, s["xt_lo"], st.times(4, 1, 3 + k))
                else:
                    wait(pe, s["vs_ready"], st.times(4, 2, k - 1))
                for ul in range(4):
                    u = 4 * k + ul
                    last = nc.tensor.transpose(ps_t[:, k % 2, P * ul:P * ul + P],
                                               kt[:, 8 * u:8 * u + 8, :].rearrange("p t h -> p (t h)"), ident[:, :])
                last.then_inc(s["v_ps"], 1)

            def scores_wait(st, g):
                if g == 0:
                    pe.wait_ge(s["kt_ready"], st.times(4, 2, 4))
                wait(pe, s["s_read"], st.times(4, 2, g - 1))

            def scores(st, g):
                for u in range(U):
                    for q in range(Q):
                        t = 8 * u + 2 * q
                        rows = kt[32 * g:32 * g + 32, t:t + 2, :].rearrange("p t h -> p (t h)")
                        last = nc.tensor.matmul(ps_s[32 * q:32 * q + 32, g % 2, 32 * u:32 * u + 32], rows, rows,
                                                start=True, stop=True)
                last.then_inc(s["s_ps"], 1)

            def x_transposes(st, c):
                if c == 0:
                    pe.wait_ge(x_ready[st.j], (st.lap + 1) * DMA)
                if c >= 2:
                    pe.wait_ge(s["xt_lo"], st.times(4, 0, c - 1))
                elif st.sv:
                    pe.wait_ge(s["vs_ready"], st.times(4, 2, 3 + c))
                else:
                    wait(pe, s["xt_lo"], st.times(4, 1, 3 + c))
                for g in range(G):
                    last = nc.tensor.transpose(ps_t[:, c % 2, P * g:P * g + P],
                                               xs[:, st.j, g, P * c:P * c + P], ident[:, :])
                last.then_inc(s["xt_ps"], 1)

            def product(bank, weight, w_cols, data, d_cols, weight_stationary, split_until=None):
                terms = [(a, b, i) for i in range(C) for a, b in ((0, 0), (0, 1), (1, 0))]
                for n, (a, b, i) in enumerate(terms):
                    w, d = weight[:, a, i, w_cols], data[:, b, i, d_cols]
                    if split_until and n % 3 == 0:
                        lo_ready, count = split_until
                        pe.wait_ge(lo_ready, count(i + 1))
                    stationary, moving = (w, d) if weight_stationary else (d, w)
                    last = nc.tensor.matmul(bank, stationary, moving, start=(n == 0), stop=(n == len(terms) - 1))
                return last

            def k_projection(st, c):
                if c >= 2:
                    pe.wait_ge(s["ks_ready"], st.times(4, 1, c - 1))
                elif st.first(4):
                    wait(pe, s["ks_ready"], st.times(4, 2, 3 + c))
                else:
                    pe.wait_ge(s["yo_ready"], st.times(4, 4, 3 + c))
                product(ps_p[:, c % 2, :], wk, slice(P * c, P * c + P), xt, slice(0, N), True,
                        (s["xt_lo"], lambda n: st.times(4, 1, n)) if c == 0 else None).then_inc(s["k_ps"], 1)

            def o_projection(st, g):
                if g < 2 and st.k:
                    pe.wait_ge(s["ks_ready"], st.times(4, 1, 3 + g))
                else:
                    wait(pe, s["yo_ready"], st.times(4, 3, g - 1))
                if st.last:
                    pe.wait_ge(s["os_lo"], st.times(4, 3, g + 1))
                product(ps_p[:, g % 2, :], wo, slice(0, F), os_, slice(P * g, P * g + P), False,
                        (s["os_lo"], lambda n: st.times(4, 3, n)) if g == 0 and not st.last else None
                        ).then_inc(s["o_ps"], 1)

            def step(st):
                if st.k:
                    k_projection(st, 0)
                if st.k_first:
                    for c in range(1, 4):
                        if c == 3:
                            scores_wait(st, 0)
                        k_projection(st, c)
                elif st.cd:
                    for k in range(4):
                        if st.sv and k == 3:
                            scores_wait(st, 0)
                        attention_out(st, k)
                elif st.sv:
                    scores_wait(st, 0)
                for g in range(4):
                    if st.sv:
                        scores(st, g)
                        if g < G - 1:
                            scores_wait(st, g + 1)
                        v_rows(st, g)
                    if st.k and g < C - 1 and not st.k_first:
                        k_projection(st, g + 1)
                for g in range(4):
                    if st.cd:
                        o_projection(st, g)
                    if st.t:
                        x_transposes(st, g)

            def styles(aff, bank, sem):
                for c in range(C):
                    for k in range(SC):
                        last = nc.tensor.matmul(bank[:, B * c:B * c + B], aff[:, k, P * c:P * c + P], cond[:, k, :],
                                                start=(k == 0), stop=(k == SC - 1))
                last.then_inc(s[sem], 1)

            def setup_style_k():
                pe.wait_ge(s["style_loaded"], 3 * DMA)
                styles(aff_k, ps_s[:, 0, :], "style_k_ps")
                pe.wait_ge(s["ident_loaded"], DMA)

            def setup_demod_k():
                pe.wait_ge(s["factors_k"], 2)
                pe.wait_ge(s["wk_squared"], 1)
                for c in range(C):
                    for k in range(C):
                        last = nc.tensor.matmul(ps_s[:, 1, B * c:B * c + B], wk_sq[:, k, P * c:P * c + P],
                                                style_sq[:, 0, k, :], start=(k == 0), stop=(k == C - 1))
                last.then_inc(s["var_k_ps"], 1)
                pe.wait_ge(s["wk_lo"], 1)

            def setup_o():
                pe.wait_ge(s["wo_loaded"], 3 * DMA)
                styles(aff_o, ps_a[:, 0, :], "style_o_ps")
                pe.wait_ge(s["factors_o"], 2)
                pe.wait_ge(s["wo_squared"], 1)
                for k in range(C):
                    last = nc.tensor.matmul(ps_a[0:B, 1, :], style_sq[:, 1, k, :], wo_sq[:, k, :],
                                            start=(k == 0), stop=(k == C - 1))
                last.then_inc(s["var_o_ps"], 1)
                pe.wait_ge(s["wo_lo"], 1)

            run_steps(pe, step, [setup_style_k, setup_demod_k, setup_o])

        @block.scalar
        def _(act):
            def kt_rows(st, k):
                if k == 0:
                    act.wait_ge(s["kt_landed"], st.times(H * DMA, 2, H * DMA))
                    wait(act, s["s_ps"], st.times(4, 2))
                    wait(act, s["v_ps"], st.times(4, 2))
                nc.scalar.activation(kt[:, 32 * k:32 * k + 32, :],
                                     kt_in[:, :, 32 * k:32 * k + 32].rearrange("p h t -> p t h"),
                                     ACT.Copy).then_inc(s["kt_ready"], 1)

            def out_columns(st, k):
                if k == 0:
                    wait(act, s["oc_landed"], st.times(H * DMA, 3))
                act.wait_ge(s["av_ps"], st.times(4, 3, k + 1))
                nc.scalar.activation(ot[:, :, 32 * k:32 * k + 32],
                                     ps_a[:, k % 2, :].rearrange("p (t h) -> p h t", h=H),
                                     ACT.Copy).then_inc(s["ot_ready"], 1)

            def v_out(st, k):
                if k == 0:
                    wait(act, s["av_ps"], st.times(4, 2))
                act.wait_ge(s["v_ps"], st.times(4, 2, k + 1))
                nc.scalar.activation(vs[:, 4 * k:4 * k + 4, :], ps_t[:, k % 2, :].rearrange("p (u f) -> p u f", u=4),
                                     ACT.Copy).then_inc(s["vs_ready"], 1)

            def exps(st, g):
                act.wait_ge(s["shifted"], st.times(4, 2, g + 1))
                wait(act, s["turned"], st.times(4, 2, g - 1))
                nc.scalar.activation(pr[:, g % 2, :], sm[:, g % 2, :], ACT.Exp, scale=SCALE).then_inc(s["exp_ready"], 1)

            def spread(st, g):
                if g == 0:
                    wait(act, s["av_ps"], st.times(4, 2))
                act.wait_ge(s["turned"], st.times(4, 2, g + 1))
                for q in range(Q):
                    rows = slice(32 * q, 32 * q + 32)
                    last = nc.scalar.activation(pt[rows, g, :, 32 * q:32 * q + 32],
                                                pq[rows, g % 2, :].rearrange("p (u f) -> p u f", u=U), ACT.Copy)
                last.then_inc(s["pt_ready"], 1)

            def k_out(st, c):
                if c == 0:
                    act.wait_ge(s["cur_demod_k"], st.times(1, 1, 1))
                    wait(act, s["kt_landed"], st.times(H * DMA, 1))
                act.wait_ge(s["k_ps"], st.times(4, 1, c + 1))
                slot = (st.j - 1) % SLOTS
                nc.scalar.activation(ks[:, c, :], ps_p[:, c % 2, :], ACT.Identity, bias=k_bias[:, c:c + 1],
                                     scale=cur[:, slot, C + c:C + c + 1]).then_inc(s["ks_ready"], 1)

            def os_high(st, c):
                if c == 0:
                    act.wait_ge(s["cur_style_o"], st.times(1, 3, 1))
                    act.wait_ge(s["oc_landed"], st.times(H * DMA, 3, H * DMA))
                    wait(act, s["o_ps"], st.times(4, 3))
                slot = (st.j - 3) % SLOTS
                nc.scalar.activation(os_[:, 0, c, :], oc[:, c, :], ACT.Copy,
                                     scale=cur[:, slot, 2 * C + c:2 * C + c + 1]).then_inc(s["os_hi"], 1)

            def os_high_group(st, g):
                if g == 0:
                    act.wait_ge(s["cur_style_o"], st.times(1, 3, 1))
                    act.wait_ge(s["o_ps"], st.times(4, 3))
                act.wait_ge(group_landed[g], HC * DMA)
                slot = (st.j - 3) % SLOTS
                for c in range(C):
                    last = nc.scalar.activation(os_[:, 0, c, P * g:P * g + P], oc[:, c, P * g:P * g + P], ACT.Copy,
                                                scale=cur[:, slot, 2 * C + c:2 * C + c + 1])
                last.then_inc(s["os_hi"], 1)

            def x_high(st, c):
                if c == 0:
                    act.wait_ge(s["cur_style_k"], st.times(1, 0, 1))
                    wait(act, s["k_ps"], st.times(4, 0))
                act.wait_ge(s["xt_ps"], st.times(4, 0, c + 1))
                nc.scalar.activation(xt[:, 0, c, :], ps_t[:, c % 2, :], ACT.Copy,
                                     scale=cur[:, st.j, c:c + 1]).then_inc(s["xt_hi"], 1)

            def current(st, back, sem):
                cols = {"cur_style_k": 0, "cur_demod_k": C, "cur_style_o": 2 * C}[sem]
                nc.scalar.activation(cur[:, (st.j - back) % SLOTS, cols:cols + C],
                                     factors[:, st.batch(back), cols:cols + C], ACT.Copy).then_inc(s[sem], 1)

            def step(st):
                if st.t:
                    current(st, 0, "cur_style_k")
                if st.k:
                    current(st, 1, "cur_demod_k")
                if st.cd:
                    current(st, 3, "cur_style_o")
                if st.sv:
                    for k in range(4):
                        kt_rows(st, k)
                if st.cd:
                    for k in range(4):
                        out_columns(st, k)
                for c in range(C):
                    if st.k and (c == 0 or st.k_first):
                        k_out(st, c)
                for g in range(4):
                    if st.sv:
                        v_out(st, g)
                        exps(st, g)
                    if st.cd and g == 2:
                        for c in range(C):
                            (os_high_group if st.last else os_high)(st, c)
                    if st.k and g < C - 1 and not st.k_first:
                        k_out(st, g + 1)
                    if st.sv and 0 < g < 3:
                        spread(st, g - 1)
                if st.t:
                    x_high(st, 0)
                if st.sv:
                    spread(st, 2)
                if st.t:
                    x_high(st, 1)
                    x_high(st, 2)
                if st.sv:
                    spread(st, 3)
                if st.t:
                    x_high(st, 3)

            def setup_style_k():
                act.wait_ge(s["factors_k"], 1)

            def setup_k():
                act.wait_ge(s["wk_loaded"], 2 * DMA)
                nc.scalar.activation(wk_sq, wk_t, ACT.Square).then_inc(s["wk_squared"], 1)
                nc.scalar.activation(wk[:, 0, :, :], wk_t, ACT.Copy).then_inc(s["wk_hi"], 1)
                act.wait_ge(s["factors_k"], 3)
                nc.scalar.activation(tmp_k, var_k, ACT.Sqrt).then_inc(s["root_k"], 1)
                act.wait_ge(s["factors_k"], 8)

            def setup_o():
                act.wait_ge(s["wo_loaded"], 3 * DMA)
                nc.scalar.activation(wo_sq, wo_t[:, :, :], ACT.Square).then_inc(s["wo_squared"], 1)
                nc.scalar.activation(wo[:, 0, :, :], wo_t[:, :, :], ACT.Copy).then_inc(s["wo_hi"], 1)
                act.wait_ge(s["factors_o"], 3)
                nc.scalar.activation(tmp_o, var_o, ACT.Sqrt).then_inc(s["root_o"], 1)
                act.wait_ge(s["zeroed"], 1)

            run_steps(act, step, [setup_style_k, setup_k, setup_o])

        @block.vector
        def _(dve):
            def scores_in(st, g):
                r = g % 2
                blocks = sm[:, r, :].rearrange("p (u f) -> p u f", u=U)
                dve.wait_ge(s["s_ps"], st.times(4, 2, g + 1))
                wait(dve, s["exp_ready"], st.times(4, 2, g - 1))
                nc.vector.tensor_tensor(blocks, ps_s[:, r, :].rearrange("p (u f) -> p u f", u=U),
                                        mask[:, :].unsqueeze(1).to_broadcast([P, U, 32]), ALU.add).then_inc(s["s_read"], 1)
                dve.wait_ge(s["s_read"], st.times(4, 2, g + 1))
                nc.vector.tensor_reduce(mx[:, r, :], blocks, AX_X, ALU.max).then_inc(s["max_ready"], 1)

            def probabilities(st, g):
                r = g % 2
                blocks = pr[:, r, :].rearrange("p (u f) -> p u f", u=U)
                dve.wait_ge(s["exp_ready"], st.times(4, 2, g + 1))
                nc.vector.tensor_reduce(den[:, r, :], blocks, AX_X, ALU.add).then_inc(s["sum_ready"], 1)
                dve.wait_ge(s["sum_ready"], st.times(4, 2, g + 1))
                nc.vector.reciprocal(rden[:, r, :], den[:, r, :]).then_inc(s["inv_ready"], 1)
                dve.wait_ge(s["inv_ready"], st.times(4, 2, g + 1))
                nc.vector.tensor_tensor(blocks, blocks, rden[:, r, :].unsqueeze(2).to_broadcast([P, U, 32]),
                                        ALU.mult).then_inc(s["prob_ready"], 1)
                dve.wait_ge(s["prob_ready"], st.times(4, 2, g + 1))
                wait(dve, s["pt_ready"], st.times(4, 2, g - 1))
                nc.vector.transpose(pq[:, r, :], pr[:, r, :]).then_inc(s["turned"], 1)

            def os_low(st, c):
                slot = (st.j - 3) % SLOTS
                dve.wait_ge(s["os_hi"], st.times(4, 3, c + 1))
                nc.vector.scalar_tensor_tensor(
                    out=os_[:, 1, c, :], in0=oc[:, c, :], scalar=cur[:, slot, 2 * C + c:2 * C + c + 1],
                    in1=os_[:, 0, c, :].bitcast(F32), op0=ALU.mult, op1=ALU.subtract).then_inc(s["os_lo"], 1)

            def os_low_group(st, g):
                slot = (st.j - 3) % SLOTS
                dve.wait_ge(s["os_hi"], st.times(4, 3, g + 1))
                for c in range(C):
                    last = nc.vector.scalar_tensor_tensor(
                        out=os_[:, 1, c, P * g:P * g + P], in0=oc[:, c, P * g:P * g + P],
                        scalar=cur[:, slot, 2 * C + c:2 * C + c + 1],
                        in1=os_[:, 0, c, P * g:P * g + P].bitcast(F32), op0=ALU.mult, op1=ALU.subtract)
                last.then_inc(s["os_lo"], 1)

            def demodulated(st, g):
                if g == 0:
                    dve.wait_ge(s["demod_row"], st.times(DMA, 3, DMA))
                wait(dve, s["out_ready"], st.times(4, 3, g - 1))
                dve.wait_ge(s["o_ps"], st.times(4, 3, g + 1))
                nc.vector.tensor_tensor(yo[:, g % 2, :], ps_p[:, g % 2, :], demod_o[:, :], ALU.mult).then_inc(s["yo_ready"], 1)

            def x_low(st, c):
                dve.wait_ge(s["xt_hi"], st.times(4, 0, c + 1))
                nc.vector.scalar_tensor_tensor(out=xt[:, 1, c, :], in0=ps_t[:, c % 2, :], scalar=cur[:, st.j, c:c + 1],
                                               in1=xt[:, 0, c, :].bitcast(F32), op0=ALU.mult,
                                               op1=ALU.subtract).then_inc(s["xt_lo"], 1)

            def last_step(st):
                for g in range(G):
                    os_low_group(st, g)
                    if g > 0:
                        demodulated(st, g - 1)
                demodulated(st, G - 1)

            def step(st):
                if st.last:
                    last_step(st)
                    return
                if st.sv:
                    scores_in(st, 0)
                    scores_in(st, 1)
                    probabilities(st, 0)
                    scores_in(st, 2)
                    probabilities(st, 1)
                if st.cd:
                    for c in range(C):
                        os_low(st, c)
                if st.sv:
                    scores_in(st, 3)
                    probabilities(st, 2)
                if st.cd:
                    demodulated(st, 0)
                if st.t:
                    x_low(st, 0)
                if st.cd:
                    demodulated(st, 1)
                if st.sv:
                    probabilities(st, 3)
                if st.t:
                    x_low(st, 1)
                if st.cd:
                    demodulated(st, 2)
                if st.t:
                    x_low(st, 2)
                    x_low(st, 3)
                if st.cd:
                    demodulated(st, 3)


            def style(m, bank, sem):
                dst = factors[:, :, 2 * m * C:(2 * m + 1) * C].rearrange("p b c -> p c b")
                nc.vector.tensor_tensor(dst, bank[:, 0:C * B].rearrange("p (c b) -> p c b", c=C),
                                        aff_b[:, m, :].unsqueeze(2).to_broadcast([P, C, B]), ALU.add).then_inc(s[sem], 1)
                dve.wait_ge(s[sem], 1)
                nc.vector.tensor_tensor(style_sq[:, m, :, :], dst, dst, ALU.mult).then_inc(s[sem], 1)

            def inverse_root(var, inv, tmp, sem, root):
                dve.wait_ge(s[root], 1)
                nc.vector.reciprocal(inv, tmp).then_inc(s[sem], 1)
                dve.wait_ge(s[sem], 4)
                nc.vector.tensor_tensor(tmp, inv, inv, ALU.mult).then_inc(s[sem], 1)
                dve.wait_ge(s[sem], 5)
                nc.vector.scalar_tensor_tensor(out=tmp, in0=tmp, scalar=-0.5, in1=var,
                                               op0=ALU.mult, op1=ALU.mult).then_inc(s[sem], 1)
                dve.wait_ge(s[sem], 6)
                nc.vector.scalar_tensor_tensor(out=inv, in0=tmp, scalar=1.5, in1=inv,
                                               op0=ALU.add, op1=ALU.mult).then_inc(s[sem], 1)

            def setup_style_k():
                dve.wait_ge(s["style_k_ps"], 1)
                style(0, ps_s[:, 0, :], "factors_k")

            def setup_k():
                dve.wait_ge(s["wk_hi"], 1)
                nc.vector.tensor_tensor(wk[:, 1, :, :], wk_t, wk[:, 0, :, :].bitcast(F32),
                                        ALU.subtract).then_inc(s["wk_lo"], 1)
                dve.wait_ge(s["var_k_ps"], 1)
                nc.vector.tensor_scalar(var_k, ps_s[:, 1, 0:C * B], EPS, None, ALU.add).then_inc(s["factors_k"], 1)
                inverse_root(var_k, inv_k, tmp_k, "factors_k", "root_k")
                dve.wait_ge(s["factors_k"], 7)
                nc.vector.tensor_copy(factors[:, :, C:2 * C].rearrange("p b c -> p c b"),
                                      inv_k.rearrange("p (c b) -> p c b", c=C)).then_inc(s["factors_k"], 1)

            def setup_o():
                dve.wait_ge(s["style_o_ps"], 1)
                style(1, ps_a[:, 0, :], "factors_o")
                dve.wait_ge(s["wo_hi"], 1)
                nc.vector.tensor_tensor(wo[:, 1, :, :], wo_t[:, :, :], wo[:, 0, :, :].bitcast(F32),
                                        ALU.subtract).then_inc(s["wo_lo"], 1)
                dve.wait_ge(s["var_o_ps"], 1)
                nc.vector.tensor_scalar(var_o, ps_a[0:B, 1, :], EPS, None, ALU.add).then_inc(s["factors_o"], 1)
                inverse_root(var_o, inv_o, tmp_o, "factors_o", "root_o")
                dve.wait_ge(s["consts_loaded"], 2 * DMA)

            run_steps(dve, step, [setup_style_k, setup_k, setup_o])

        @block.gpsimd
        def _(pool):
            def shift(st, g):
                r = g % 2
                blocks = sm[:, r, :].rearrange("p (u f) -> p u f", u=U)
                pool.wait_ge(s["max_ready"], st.times(4, 2, g + 1))
                nc.gpsimd.tensor_tensor(blocks, blocks, mx[:, r, :].unsqueeze(2).to_broadcast([P, U, 32]),
                                        ALU.subtract).then_inc(s["shifted"], 1)

            def step(st):
                if st.sv:
                    for g in range(G):
                        shift(st, g)
                if st.cd:
                    for g in range(G):
                        if g == 0:
                            pool.wait_ge(s["x_bias_ready"], st.times(1, 3, 1))
                        pool.wait_ge(s["yo_ready"], st.times(4, 3, g + 1))
                        rows = xs[:, (st.j - 3) % SLOTS, g, :]
                        nc.gpsimd.tensor_tensor(rows, rows, yo[:, g % 2, :], ALU.add).then_inc(s["out_ready"], 1)
                if st.t:
                    pool.wait_ge(s["xt_ps"], st.times(4, 0, 4))
                    rows = xs[:, st.j, :, :]
                    nc.gpsimd.tensor_tensor(rows, rows, o_bias[:, :].unsqueeze(1).to_broadcast([P, G, F]),
                                            ALU.add).then_inc(s["x_bias_ready"], 1)

            def setup_bias():
                pool.wait_ge(s["consts_loaded"], 2 * DMA)

            def setup_zeros():
                pool.wait_ge(s["wk_lo"], 1)
                pool.wait_ge(s["var_k_ps"], 1)
                nc.gpsimd.memset(pt[:, :, :, :], 0.0).then_inc(s["zeroed"], 1)

            run_steps(pool, step, [setup_bias, setup_zeros])


def kernel(x, cond_512, L0_cond_k_aff_w, L0_cond_k_aff_b, L0_cond_k_w, L0_cond_k_b,
           L0_cond_o_aff_w, L0_cond_o_aff_b, L0_cond_o_w, L0_cond_o_b):
    import numpy as np
    import concourse.bacc as bacc
    from concourse.bass_utils import run_bass_kernel_spmd

    def columns(v):
        return np.ascontiguousarray(np.asarray(v).reshape(C, P).T)

    token = np.arange(P)[:, None] % 32 // H
    arrays = {
        "x": np.ascontiguousarray(x),
        "cond_t": np.ascontiguousarray(np.asarray(cond_512).T),
        "k_aff_t": np.ascontiguousarray(np.asarray(L0_cond_k_aff_w).T),
        "k_aff_b": columns(L0_cond_k_aff_b),
        "k_w_t": np.ascontiguousarray(np.asarray(L0_cond_k_w).T),
        "k_b": columns(L0_cond_k_b),
        "o_aff_t": np.ascontiguousarray(np.asarray(L0_cond_o_aff_w).T),
        "o_aff_b": columns(L0_cond_o_aff_b),
        "o_w_t": np.ascontiguousarray(np.asarray(L0_cond_o_w).T),
        "o_b": np.ascontiguousarray(L0_cond_o_b),
        "ident": np.eye(P, dtype=np.float32),
        "mask": np.where(token == np.arange(32)[None, :] // H, 0.0, -1e30).astype(np.float32),
    }
    nc = bacc.Bacc("TRN2", target_bir_lowering=False, num_devices=1)
    args = [nc.dram_tensor(f"in_{name}", a.shape, F32, kind="ExternalInput").ap() for name, a in arrays.items()]
    out = nc.dram_tensor("out", (B, N, F), F32, kind="ExternalOutput").ap()
    demod_dram = nc.dram_tensor("demod_dram", (B, F), F32, kind="Internal").ap()
    build(nc, *args, out, demod_dram)
    got = run_bass_kernel_spmd(nc, [{f"in_{k}": a for k, a in arrays.items()}], core_ids=[0])
    return got.results[0]["out"]
```
